# Optimizing a Trainium2 kernel written in Bass

```python
import numpy as np
import jax
import jax.numpy as jnp

def _softmax(x, axis=-1):
    return jax.nn.softmax(x, axis=axis)

def _gelu(x):
    return jax.nn.gelu(x, approximate=True)

def _silu(x):
    return jax.nn.silu(x)

def _sigmoid(x):
    return jax.nn.sigmoid(x)

def _layernorm(x, axis=-1, eps=1e-05):
    m = jnp.mean(x, axis=axis, keepdims=True)
    v = jnp.var(x, axis=axis, keepdims=True)
    return (x - m) / jnp.sqrt(v + eps)

def _scatter_add(tgt, idx, src, axis=0):
    return tgt.at[idx].add(src)

def _segment_sum(src, seg, n):
    return jax.ops.segment_sum(src, seg, n)
kernel_name = 'mk_seq_preln_d1_jaxref_r4_bb7288'

def setup_inputs(seed: int=0):
    np.random.seed(seed)
    _w = jnp.asarray

    def _L0_attn_setup():
        import jax, jax.numpy as jnp
        import numpy as np
        import math
        IN_DIM = 256
        LATENT_DIM = 64
        OUT_DIM = 256

        def _kaiming(key, fan_out, fan_in):
            std = math.sqrt(2.0 / fan_in)
            return jax.random.normal(key, (fan_out, fan_in), dtype=jnp.float32) * std
        key = jax.random.key(seed)
        kx, kt, kp, kg = jax.random.split(key, 4)
        x = jax.random.normal(kx, (8, 1024, IN_DIM), dtype=jnp.float32)
        W_theta = _kaiming(kt, LATENT_DIM, IN_DIM)
        W_phi = _kaiming(kp, LATENT_DIM, IN_DIM)
        W_g = _kaiming(kg, OUT_DIM, IN_DIM)
        return {'x': x, 'W_theta': W_theta, 'W_phi': W_phi, 'W_g': W_g}
    _L0_attn_in = _L0_attn_setup()

    def _L0_ffn_setup():
        import jax, jax.numpy as jnp
        import numpy as np
        HID = 256
        NH = 16
        NKV = 4
        HD = HID // NH
        E = 8
        TOPK = 2
        FFN = 512
        EPS = 1e-05
        THETA = 10000.0

        def _rmsnorm(x, w):
            var = jnp.mean(x * x, axis=-1, keepdims=True)
            return x * jax.lax.rsqrt(var + EPS) * w

        def _rope_tables(S):
            inv_freq = 1.0 / THETA ** (jnp.arange(0, HD, 2, dtype=jnp.float32) / HD)
            freqs = jnp.arange(S, dtype=jnp.float32)[:, None] * inv_freq[None, :]
            emb = jnp.concatenate([freqs, freqs], axis=-1)
            return (jnp.cos(emb), jnp.sin(emb))

        def _apply_rope(t, cos, sin):
            t1, t2 = jnp.split(t, 2, axis=-1)
            rot = jnp.concatenate([-t2, t1], axis=-1)
            return t * cos[None, :, None, :] + rot * sin[None, :, None, :]
        key = jax.random.key(seed)
        ks = jax.random.split(key, 6)
        B, S = (1, 512)
        x = jax.random.normal(ks[0], (B, S, HID), dtype=jnp.float32)
        wqkv = jax.random.normal(ks[1], ((NH + 2 * NKV) * HD, HID), dtype=jnp.float32) * 0.02
        wo = jax.random.normal(ks[2], (HID, NH * HD), dtype=jnp.float32) * 0.02
        gate_w = jax.random.normal(ks[3], (E, HID), dtype=jnp.float32) * 0.02
        w13 = jax.random.normal(ks[4], (E, 2 * FFN, HID), dtype=jnp.float32) * 0.02
        w2 = jax.random.normal(ks[5], (E, HID, FFN), dtype=jnp.float32) * 0.02
        return {'x': x, 'ln1_w': jnp.ones((HID,), jnp.float32), 'ln2_w': jnp.ones((HID,), jnp.float32), 'wqkv': wqkv, 'wo': wo, 'gate_w': gate_w, 'w13': w13, 'w2': w2}
    _L0_ffn_in = _L0_ffn_setup()
    _d = {'L0_attn_x': _L0_attn_in['x'], 'L0_attn_W_theta': _L0_attn_in['W_theta'], 'L0_attn_W_phi': _L0_attn_in['W_phi'], 'L0_attn_W_g': _L0_attn_in['W_g'], 'L0_ffn_ln1_w': _L0_ffn_in['ln1_w'], 'L0_ffn_ln2_w': _L0_ffn_in['ln2_w'], 'L0_ffn_wqkv': _L0_ffn_in['wqkv'], 'L0_ffn_wo': _L0_ffn_in['wo'], 'L0_ffn_gate_w': _L0_ffn_in['gate_w'], 'L0_ffn_w13': _L0_ffn_in['w13'], 'L0_ffn_w2': _L0_ffn_in['w2']}
    _x0 = _d['L0_attn_x']
    _d['L0_attn_x'] = jax.random.normal(jax.random.fold_in(jax.random.key(seed), 1), (4, 1024, 256), dtype=_x0.dtype)
    del _x0
    return _d

def reference(L0_attn_x, L0_attn_W_theta, L0_attn_W_phi, L0_attn_W_g, L0_ffn_ln1_w, L0_ffn_ln2_w, L0_ffn_wqkv, L0_ffn_wo, L0_ffn_gate_w, L0_ffn_w13, L0_ffn_w2):

    def _L0_attn_ref(x, W_theta, W_phi, W_g):
        import jax, jax.numpy as jnp
        import numpy as np
        import math
        IN_DIM = 256
        LATENT_DIM = 64
        OUT_DIM = 256

        def _kaiming(key, fan_out, fan_in):
            std = math.sqrt(2.0 / fan_in)
            return jax.random.normal(key, (fan_out, fan_in), dtype=jnp.float32) * std
        theta_x = jnp.einsum('bnf,lf->bnl', x, W_theta)
        phi_x = jnp.einsum('bnf,lf->bnl', x, W_phi)
        fun_g_x = jnp.einsum('bnf,of->bno', x, W_g)
        scale = 1.0 / math.sqrt(IN_DIM)
        att = jnp.einsum('bnl,bml->bnm', theta_x, phi_x) * scale
        return jnp.einsum('bnm,bmo->bno', att, fun_g_x)

    def _L0_ffn_ref(x, ln1_w, ln2_w, wqkv, wo, gate_w, w13, w2):
        import jax, jax.numpy as jnp
        import numpy as np
        HID = 256
        NH = 16
        NKV = 4
        HD = HID // NH
        E = 8
        TOPK = 2
        FFN = 512
        EPS = 1e-05
        THETA = 10000.0

        def _rmsnorm(x, w):
            var = jnp.mean(x * x, axis=-1, keepdims=True)
            return x * jax.lax.rsqrt(var + EPS) * w

        def _rope_tables(S):
            inv_freq = 1.0 / THETA ** (jnp.arange(0, HD, 2, dtype=jnp.float32) / HD)
            freqs = jnp.arange(S, dtype=jnp.float32)[:, None] * inv_freq[None, :]
            emb = jnp.concatenate([freqs, freqs], axis=-1)
            return (jnp.cos(emb), jnp.sin(emb))

        def _apply_rope(t, cos, sin):
            t1, t2 = jnp.split(t, 2, axis=-1)
            rot = jnp.concatenate([-t2, t1], axis=-1)
            return t * cos[None, :, None, :] + rot * sin[None, :, None, :]
        B, S, _ = x.shape
        h = _rmsnorm(x, ln1_w)
        qkv = jnp.einsum('bsh,oh->bso', h, wqkv)
        q = qkv[..., :NH * HD].reshape(B, S, NH, HD)
        k = qkv[..., NH * HD:(NH + NKV) * HD].reshape(B, S, NKV, HD)
        v = qkv[..., (NH + NKV) * HD:].reshape(B, S, NKV, HD)
        cos, sin = _rope_tables(S)
        q = _apply_rope(q, cos, sin)
        k = _apply_rope(k, cos, sin)
        groups = NH // NKV
        k = jnp.repeat(k, groups, axis=2)
        v = jnp.repeat(v, groups, axis=2)
        scale = HD ** (-0.5)
        scores = jnp.einsum('bqhd,bkhd->bhqk', q, k) * scale
        causal = jnp.tril(jnp.ones((S, S), dtype=bool))
        scores = jnp.where(causal[None, None], scores, jnp.finfo(scores.dtype).min)
        probs = jax.nn.softmax(scores, axis=-1)
        attn = jnp.einsum('bhqk,bkhd->bqhd', probs, v).reshape(B, S, NH * HD)
        x = x + jnp.einsum('bso,ho->bsh', attn, wo)
        h = _rmsnorm(x, ln2_w).reshape(-1, HID)
        T = h.shape[0]
        logits = jnp.einsum('th,eh->te', h, gate_w)
        rprobs = jax.nn.softmax(logits.astype(jnp.float32), axis=-1)
        topw, topi = jax.lax.top_k(rprobs, TOPK)
        topw = topw / jnp.sum(topw, axis=-1, keepdims=True)
        wfull = jnp.zeros((T, E), jnp.float32).at[jnp.arange(T)[:, None], topi].set(topw)
        wfull = wfull.astype(h.dtype)
        out = jnp.zeros((T, HID), h.dtype)
        for e in range(E):
            w1 = w13[e, :FFN]
            w3 = w13[e, FFN:]
            g = jax.nn.silu(h @ w1.T) * (h @ w3.T)
            out = out + jnp.einsum('tf,hf->th', g, w2[e]) * wfull[:, e:e + 1]
        return x + out.reshape(B, S, HID)
    x = L0_attn_x
    x = x + _L0_attn_ref(_layernorm(x, axis=-1), L0_attn_W_theta, L0_attn_W_phi, L0_attn_W_g)
    x = x + _L0_ffn_ref(_layernorm(x, axis=-1), L0_ffn_ln1_w, L0_ffn_ln2_w, L0_ffn_wqkv, L0_ffn_wo, L0_ffn_gate_w, L0_ffn_w13, L0_ffn_w2)
    return x

_drawn_inputs = setup_inputs


def setup_inputs(seed=0):
    import zlib

    import numpy as np

    out = dict(_drawn_inputs(seed))
    spreads = {'L0_ffn_ln1_w': (1.0, 0.6), 'L0_ffn_ln2_w': (1.0, 0.6)}
    factors = {'L0_ffn_wqkv': 8.0,
     'L0_ffn_wo': 8.0,
     'L0_ffn_gate_w': 8.0,
     'L0_ffn_w13': 8.0,
     'L0_ffn_w2': 8.0}
    for name, (base, spread) in spreads.items():
        noise = np.random.default_rng([zlib.crc32(name.encode()), seed]).standard_normal(out[name].shape)
        drawn = base * np.exp(spread * noise) if base else spread * noise
        out[name] = jnp.asarray(drawn.astype(out[name].dtype))
    for name, factor in factors.items():
        out[name] = (out[name] * factor).astype(out[name].dtype)
    return out
```

```python
from contextlib import ExitStack

import numpy as np

import concourse.bass as bass
from concourse import mybir

F32 = mybir.dt.float32
BF16 = mybir.dt.bfloat16
I32 = mybir.dt.int32
ALU = mybir.AluOpType
ACT = mybir.ActivationFunctionType
AX = mybir.AxisListType

P = 128
NBATCH, SEQ, D = 4, 1024, 256
KD = D // P
TPB = SEQ // P
NTILE = NBATCH * TPB
LATENT = 64
NH, NKV, HD = 16, 4, 16
GRP = NH // NKV
QK = (NH + NKV) * HD
QKV = (NH + 2 * NKV) * HD
NE, TOPK, FFN = 8, 2, 512
KF = FFN // P
EPS = 1e-5
CH = 512
QR = SEQ // CH
TPR = CH // P
THETA = 10000.0

QPART = (0, 0, 0, 1, 1, 2)
KPART = (0, 1, 2, 0, 1, 0)
STACK = len(QPART) * HD
NMAX = 2
MASKED = -1e38

GROUPS = ((0, 1, 2), (3,))
RW = D + 2
NOWHERE = 1 << 20


def n_blocks(batches):
    return (TOPK * len(batches) * SEQ + NE * (P - 1)) // P


class Engine:

    def __init__(self, make):
        self.make, self.steps, self.count, self.waited = make, [], {}, {}
        self.latest = None

    def wait(self, *ticks):
        for t in ticks:
            if t is not None and self.waited.get(t[0], 0) < t[1]:
                self.waited[t[0]] = t[1]
                self.steps.append(lambda e, t=t: e.wait_ge(self.make(t[0]), t[1]))

    def run(self, fn, after=(), done=None):
        self.wait(*after)
        if done is None:
            self.steps.append(fn)
            return None
        self.count[done] = self.count.get(done, 0) + 1
        self.steps.append(lambda e: fn(e).then_inc(self.make(done), 1))
        self.latest = (done, self.count[done])
        return self.latest

    def play(self, e):
        for s in self.steps:
            s(e)


class Loads:

    def __init__(self, engine, name, depth):
        self.engine, self.name, self.depth, self.n = engine, name, depth, 0
        self.sent = [0] * depth

    def start(self, *fns, after=()):
        i = self.n % self.depth
        self.n += 1
        sem = f"{self.name}{i}"
        if self.sent[i]:
            self.engine.wait((sem, self.sent[i]))
        self.engine.wait(*after)
        for fn in fns:
            self.engine.steps.append(lambda e, fn=fn: fn(e).then_inc(self.engine.make(sem), 16))
        self.sent[i] += 16 * len(fns)
        return (sem, self.sent[i])

    def all_landed(self):
        return [(f"{self.name}{i}", n) for i, n in enumerate(self.sent) if n]


class Ring:

    def __init__(self, buffers):
        self.buffers, self.n = buffers, 0
        self.free = [()] * len(buffers)

    def take(self):
        i = self.n % len(self.buffers)
        self.n += 1
        return i, self.buffers[i], self.free[i]

    def release(self, i, *ticks):
        self.free[i] = ticks


def mega_kernel(nc, x, wtheta, wphi, wgT, ln1, ln2, wqkvT, wrotT, woT, gateT, w13T, w2T,
                cos_t, sin_t, eye, tri, ids, out):
    with ExitStack() as ctx:
        sems = {}

        def make(name):
            if name not in sems:
                sems[name] = ctx.enter_context(nc.semaphore(name))
            return sems[name]

        def sb(name, shape, dt=F32):
            return ctx.enter_context(nc.sbuf_tensor(name, shape, dt))[:]

        pe, act, dve, pool, sp = (Engine(make) for _ in range(5))
        load = Loads(sp, "load", 8)
        split_store = Loads(sp, "split_store", 4)
        stack_load = Loads(sp, "stack_load", 2)
        max_load = Loads(sp, "max_load", 2)
        pack_move = Loads(sp, "pack_move", 3)
        base_store = Loads(sp, "base_store", 4)
        weight_load = Loads(sp, "weight_load", 4)
        block_load = Loads(sp, "block_load", 4)
        pad_store = Loads(sp, "pad_store", 2)
        scatter = Loads(pool, "scatter", 6)
        add_out = Loads(pool, "add_out", 1)

        w13_mem = sb("w13_mem", [P, KD * NE * 2 * FFN])
        w2_mem = sb("w2_mem", [P, NE * KF * D])

        def carve(mem, sizes):
            at, views = 0, []
            for n in sizes:
                views.append(mem[:, at:at + n])
                at += n
            assert at <= mem.shape[1], (at, mem.shape)
            return views

        def grid(view, a):
            return view.rearrange("p (a b) -> p a b", a=a)

        (xn_f, xnT_f, h_f, hT_f, gram_f, gw_f, mix_f, cosT, sinT, rot1, rot2, qk32, qres, split_f) = carve(
            w13_mem, [TPB * D, KD * SEQ, TPB * D, KD * SEQ, KD * D, KD * D, KD * D, SEQ, SEQ, CH, CH, CH, CH, 2 * 3 * CH // 2])
        xn, xnT, h, hT = grid(xn_f, TPB), grid(xnT_f, KD), grid(h_f, TPB), grid(hT_f, KD)
        gram, gw, mix = grid(gram_f, KD), grid(gw_f, KD), grid(mix_f, KD)
        splits = Ring([s.rearrange("p (s q) -> p s q", s=3) for s in (
            split_f.bitcast(BF16)[:, 0:3 * CH], split_f.bitcast(BF16)[:, 3 * CH:6 * CH])])
        (wgT_f, pair_f, wqkv_f, wrot_f, x_even, v_even, route_a) = carve(
            w2_mem, [KD * D, KD * D, KD * QKV, KD * QK, TPB * D, TPB * NKV * 32, 1700])
        wgT_s, pairT, wqkv_s, wrot_s = grid(wgT_f, KD), grid(pair_f, KD), grid(wqkv_f, KD), grid(wrot_f, KD)
        x1 = [grid(x_even, TPB), grid(sb("x_odd", [P, TPB * D]), TPB)]
        v1_flat = [v_even, sb("v_odd", [P, TPB * NKV * 32])]
        v1 = [v.rearrange("p (t g c) -> p t g c", t=TPB, g=NKV) for v in v1_flat]

        w13_s = w13_mem.rearrange("p (k n) -> p k n", k=KD)
        stack_mem = sb("stack_mem", [P, 2 * (GRP + 1) * SEQ // 2])
        stack = [s.rearrange("p (h t) -> p h t", h=GRP + 1) for s in (
            stack_mem.bitcast(BF16)[:, 0:(GRP + 1) * SEQ], stack_mem.bitcast(BF16)[:, (GRP + 1) * SEQ:])]
        probs_mem = sb("probs_mem", [P, 2 * GRP * CH])
        probs = Ring([p.rearrange("p (h q) -> p h q", h=GRP) for p in (probs_mem[:, 0:GRP * CH], probs_mem[:, GRP * CH:])])
        hrow = sb("hrow", [P, NTILE * RW]).rearrange("p (t c) -> p t c", t=NTILE)
        attnT = sb("attnT", [P, KD * SEQ]).rearrange("p (k t) -> p k t", k=KD)
        onorm = sb("onorm", [P, CH])
        osum = sb("osum", [P, CH])
        yrow = sb("yrow", [P, D])
        wo_s = sb("wo_s", [P, KD * D]).rearrange("p (k n) -> p k n", k=KD)
        gate_s = sb("gate_s", [P, KD * NE]).rearrange("p (k n) -> p k n", k=KD)
        ln1_s = sb("ln1_s", [P, KD])
        ln2_s = sb("ln2_s", [P, D])
        ident = sb("ident", [P, P])
        identb = sb("identb", [P, P], BF16)
        causal = sb("causal", [P, P], BF16)
        before = sb("before", [P, P], BF16)
        onesb = sb("onesb", [P, P], BF16)
        st = sb("st", [P, TPB * 6]).rearrange("p (t c) -> p t c", t=TPB)
        mv = sb("mv", [P, TPB * 2]).rearrange("p (t c) -> p t c", t=TPB)
        rt = sb("rt", [P, 6 * TPB]).rearrange("p (a t) -> p a t", a=6)
        rstd, mean1, scale1 = (sb(n, [P, 2 * TPB]).rearrange("p (b t) -> p b t", b=2) for n in ("rstd", "mean1", "scale1"))
        rstd2 = sb("rstd2", [P, TPB])
        mx = sb("mx", [P, 2 * 16]).rearrange("p (c n) -> p c n", c=2)
        mxc = sb("mxc", [P, 16])
        mneg = sb("mneg", [16, P])
        mneg_parts = sb("mneg_parts", [16, NMAX * P], BF16).rearrange("p (s q) -> p s q", s=NMAX)
        mres = sb("mres", [16, P])
        h2T = sb("h2T", [P, KD * P]).rearrange("p (k t) -> p k t", k=KD)
        logits = sb("logits", [P, NTILE * NE]).rearrange("p (t e) -> p t e", t=NTILE)
        ids_s = sb("ids_s", [P, NTILE], I32)

        bank = [ctx.enter_context(nc.psum_tensor(f"bank{i}", [P, CH], F32))[:] for i in range(8)]
        max_banks = Ring([bank[0], bank[1]])
        score_banks = Ring([bank[2], bank[3], bank[4]])
        pv_bank = Ring([bank[5]])
        misc = Ring([bank[6], bank[7]])

        parts = [nc.dram_tensor(f"qk_parts{b}", [3, QK, SEQ], BF16, kind="Internal").ap() for b in range(NBATCH)]
        rows = [nc.dram_tensor(f"routed{i}", [n_blocks(g) * P, RW], F32, kind="Internal").ap() for i, g in enumerate(GROUPS)]
        x_v = x.rearrange("b (j p) d -> b p j d", p=P)
        out_t = out.rearrange("b (j p) d -> (b j) p d", p=P)
        out_rows = out.rearrange("b n d -> (b n) d")

        def kview(w):
            return w.rearrange("(k p) n -> p k n", p=P)

        x_tick = {0: load.start(lambda e: e.dma_start(x1[0], x_v[0]))}
        eye_t = load.start(lambda e: e.dma_start(ident, eye))
        wt_f, wp_f = h_f[0:LATENT, 0:D], h_f[0:LATENT, D:2 * D]
        tp_t = [load.start(lambda e: e.dma_start(wt_f, wtheta)), load.start(lambda e: e.dma_start(wp_f, wphi))]
        wg_t = load.start(lambda e: e.dma_start(wgT_s, kview(wgT)))
        wqkv_t = [load.start(lambda e: e.dma_start(wqkv_s, kview(wqkvT))),
                  load.start(lambda e: e.dma_start(wrot_s, kview(wrotT))),
                  load.start(lambda e: e.dma_start(ln1_s, ln1.rearrange("(k p) -> p k", p=P), allow_slow_non_contiguous=True))]
        rope_t = [load.start(lambda e: e.dma_start(cosT, cos_t)), load.start(lambda e: e.dma_start(sinT, sin_t))]
        tri_in = osum[:, 0:2 * P]
        tri_t = load.start(lambda e: e.dma_start(tri_in.rearrange("p (a b) -> p a b", a=2), tri))
        ids_t = load.start(lambda e: e.dma_start(ids_s, ids))
        ln2_t = load.start(lambda e: e.dma_start(ln2_s, ln2.partition_broadcast(P)))
        wo_t = load.start(lambda e: e.dma_start(wo_s, kview(woT)))
        gate_t = load.start(lambda e: e.dma_start(gate_s, kview(gateT)))
        x_tick[1] = load.start(lambda e: e.dma_start(x1[1], x_v[1]))

        def pool_set(fn, after=()):
            n = pool.count.get("pool_set", 0)
            return pool.run(fn, after=[*after, ("pool_set", n)], done="pool_set")

        pad = xnT_f[:, 0:RW]
        pool_set(lambda e: e.memset(pad, 0.0))
        pad_set = pool_set(lambda e: e.memset(pad.bitcast(I32)[:, D:D + 1], NOWHERE))
        for v in v1_flat:
            pool_set(lambda e, v=v: e.memset(v, 0.0))
        for v in v1:
            v_set = pool_set(lambda e, v=v: e.memset(v[:, :, :, HD:HD + 1], 1.0))
        for s in stack:
            ones_set = pool_set(lambda e, s=s: e.memset(s[STACK:STACK + NMAX, GRP, :], 1.0))
        pads = [pad_store.start(lambda e, r=r: e.dma_start(
            r.rearrange("(n p) c -> p n c", p=P), pad.unsqueeze(1).broadcast_to([P, r.shape[0] // P, RW])), after=[pad_set]) for r in rows]
        hrow_i = hrow.bitcast(I32)
        ids_set = pool_set(lambda e: e.tensor_copy(hrow_i[:, :, D], ids_s), after=[ids_t])
        iota = sb("iota", [P, 96])
        iota128 = sb("iota128", [P, NTILE])
        onesf = sb("onesf", [P, NTILE])
        pool_set(lambda e: e.iota(iota, pattern=[[1, 96]], base=0, channel_multiplier=0, allow_small_or_imprecise_dtypes=True))
        pool_set(lambda e: e.iota(iota128, pattern=[[P, NTILE]], base=0, channel_multiplier=0, allow_small_or_imprecise_dtypes=True))
        iota_t = pool_set(lambda e: e.memset(onesf, 1.0))

        dve.run(lambda e: e.tensor_copy(identb, ident), after=[eye_t], done="dve_const")
        dve.run(lambda e: e.tensor_scalar(causal, tri_in[:, 0:P], MASKED, None, ALU.mult), after=[tri_t], done="dve_const")
        dve.run(lambda e: e.tensor_copy(before, tri_in[:, P:2 * P]), done="dve_const")
        const_t = dve.run(lambda e: e.memset(onesb, 1.0), done="dve_const")
        for k in range(KD):
            dve.run(lambda e, k=k: e.tensor_scalar(wqkv_s[:, k], wqkv_s[:, k], ln1_s[:, k:k + 1], None, ALU.mult), after=wqkv_t, done="dve_wqkv")
            wq_ready = dve.run(lambda e, k=k: e.tensor_scalar(wrot_s[:, k], wrot_s[:, k], ln1_s[:, k:k + 1], None, ALU.mult), done="dve_wqkv")

        i, bk, free = misc.take()

        def pair_mm(e, bk=bk):
            for k in range(KD):
                m = e.matmul(bk[:, k * D:(k + 1) * D], wp_f[:, k * P:(k + 1) * P], wt_f, start=True, stop=True)
            return m
        t = pe.run(pair_mm, after=tp_t, done="pe_pair")
        pair_ready = act.run(lambda e, bk=bk: e.activation(pairT, grid(bk, KD), ACT.Copy, scale=float(D) ** -0.5), after=[t], done="act_pair")
        misc.release(i, pair_ready)

        def dchain(fns, after, name):
            t = None
            for f in fns:
                t = dve.run(f, after=[*after, t] if t else after, done=name)
            return t

        def rsqrt_steps(dst, var, a, u, w):
            ai, ui, di = a.bitcast(I32), u.bitcast(I32), dst.bitcast(I32)
            steps = [lambda e: e.tensor_scalar(a, var, EPS, None, ALU.add),
                     lambda e: e.tensor_scalar(ui, ai, 1, None, ALU.logical_shift_right),
                     lambda e: e.tensor_scalar(di, ui, -1.0, float(0x5F3759DF), ALU.mult, ALU.add)]
            for _ in range(3):
                steps += [lambda e: e.scalar_tensor_tensor(u, dst, -0.5, a, ALU.mult, ALU.mult),
                          lambda e: e.tensor_tensor(w, u, dst, ALU.mult),
                          lambda e: e.scalar_tensor_tensor(dst, w, 1.5, dst, ALU.add, ALU.mult)]
            return steps

        def transposes(src_of, dst, n, after, released=()):
            t = None
            for i0 in range(0, n, 4):
                m = min(4, n - i0)
                i, bk, free = misc.take()

                def tr(e, i0=i0, m=m, bk=bk):
                    for c in range(m):
                        last = e.transpose(bk[:, c * P:(c + 1) * P], src_of(i0 + c), ident)
                    return last
                tt = pe.run(tr, after=[*after, *free, eye_t], done="pe_transpose")
                t = act.run(lambda e, i0=i0, m=m, bk=bk: e.activation(dst(i0, m), bk[:, 0:m * P].rearrange("p (c t) -> p c t", c=m), ACT.Copy),
                            after=[tt, *released], done="act_transpose")
                misc.release(i, t)
            return t

        x1_free = [(), ()]
        v1_free = [(), ()]
        x1_ready, v_ready, parts_ready = {}, {}, {}
        last = {}

        def project(b):
            o = b % 2
            xb = x1[o]
            if b not in x_tick:
                x_tick[b] = load.start(lambda e: e.dma_start(xb, x_v[b]), after=x1_free[o])
            for j in range(TPB):
                dve.run(lambda e, j=j: e.bn_stats(st[:, j], xb[:, j]), after=[x_tick[b], last.get("st")], done="dve_stats")
            yield
            t = ("dve_stats", dve.count["dve_stats"])
            for j in range(TPB):
                dve.run(lambda e, j=j: e.bn_aggr(mv[:, j], st[:, j]), after=[t, last.get("mv")], done="dve_aggr")
            t = last["st"] = ("dve_aggr", dve.count["dve_aggr"])
            t = dchain(rsqrt_steps(rt[:, 0], mv[:, :, 1], rt[:, 1], rt[:, 2], rt[:, 3]), [t, last.get("rt")], "dve_rsqrt")
            yield
            for j in range(TPB):
                xn_t = dve.run(lambda e, j=j: e.tensor_scalar(xn[:, j], xb[:, j], mv[:, j, 0:1], rt[:, 0, j:j + 1], ALU.subtract, ALU.mult),
                               after=[t, last.get("xn")], done="dve_xn")
            last["mv"] = last["rt"] = xn_t
            yield
            i, bk, free = misc.take()
            for k in range(KD):
                def gm(e, k=k, bk=bk):
                    for j in range(TPB):
                        m = e.matmul(bk[:, k * D:(k + 1) * D], xn[:, j, k * P:(k + 1) * P], xn[:, j], start=(j == 0), stop=(j == TPB - 1))
                    return m
                t = pe.run(gm, after=[xn_t, *free], done="pe_gram")
                yield
            gram_t = act.run(lambda e, bk=bk: e.activation(gram, grid(bk, KD), ACT.Copy), after=[t], done="act_gram")
            misc.release(i, gram_t)
            xnT_t = transposes(lambda c: xn[:, c // KD, (c % KD) * P:(c % KD + 1) * P],
                               lambda i0, m: xnT[:, :, i0 // KD * P:(i0 + m) // KD * P].rearrange("p k (j t) -> p j k t", t=P),
                               0, [xn_t])
            for c0 in range(0, TPB * KD, 4):
                i, bk, free = misc.take()

                def tr(e, c0=c0, bk=bk):
                    for c in range(4):
                        j, k = c0 // KD + c % 2, c // 2
                        m = e.transpose(bk[:, c * P:(c + 1) * P], xn[:, j, k * P:(k + 1) * P], ident)
                    return m
                tt = pe.run(tr, after=[xn_t, *free, eye_t, last.get("xnT")], done="pe_xnT")
                xnT_t = act.run(lambda e, c0=c0, bk=bk: e.activation(
                    xnT[:, :, c0 // KD * P:(c0 // KD + 2) * P], bk.rearrange("p (k t) -> p k t", k=KD), ACT.Copy), after=[tt, pads[0], pads[1]], done="act_xnT")
                misc.release(i, xnT_t)
                yield
            last["xn"] = tt

            def square(lhs, rhs, dst, after, name):
                i, bk, free = misc.take()

                def mm(e, bk=bk):
                    for r in range(KD):
                        for k in range(KD):
                            m = e.matmul(bk[:, r * D:(r + 1) * D], lhs[:, k, r * P:(r + 1) * P], rhs[:, k], start=(k == 0), stop=(k == KD - 1))
                    return m
                t = pe.run(mm, after=[*after, *free], done="pe_square")
                t = act.run(lambda e, bk=bk: e.activation(dst, grid(bk, KD), ACT.Copy), after=[t], done="act_square")
                misc.release(i, t)
                return t
            t = square(gram, wgT_s, gw, [gram_t, wg_t], "gw")
            yield
            mix_t = square(pairT, gw, mix, [t, pair_ready], "mix")
            yield
            for j0 in range(0, TPB, 2):
                i, bk, free = misc.take()

                def mm(e, j0=j0, bk=bk):
                    for c in range(2):
                        for k in range(KD):
                            m = e.matmul(bk[:, c * D:(c + 1) * D], xnT[:, k, (j0 + c) * P:(j0 + c + 1) * P], mix[:, k], start=(k == 0), stop=(k == KD - 1))
                    return m
                tt = pe.run(mm, after=[mix_t, xnT_t, *free], done="pe_x1")
                x1_t = dve.run(lambda e, j0=j0, bk=bk: e.tensor_tensor(xb[:, j0:j0 + 2], grid(bk, 2), xb[:, j0:j0 + 2], ALU.add), after=[tt], done="dve_x1")
                misc.release(i, x1_t)
                for j in (j0, j0 + 1):
                    dve.run(lambda e, j=j: e.bn_stats(st[:, j], xb[:, j]), after=[x1_t, last["st"]], done="dve_stats")
                yield
            last["xnT"] = tt
            t = ("dve_stats", dve.count["dve_stats"])
            for j in range(TPB):
                dve.run(lambda e, j=j: e.bn_aggr(mv[:, j], st[:, j]), after=[t, last["mv"]], done="dve_aggr")
            t = ("dve_aggr", dve.count["dve_aggr"])
            last["st"] = t
            steps = rsqrt_steps(rstd[:, o], mv[:, :, 1], rt[:, 1], rt[:, 2], rt[:, 3])
            steps += [lambda e: e.tensor_copy(mean1[:, o], mv[:, :, 0]),
                      lambda e: e.tensor_tensor(rt[:, 4], rstd[:, o], rstd[:, o], ALU.mult),
                      lambda e: e.tensor_tensor(rt[:, 4], rt[:, 4], mv[:, :, 1], ALU.mult)]
            steps += rsqrt_steps(rt[:, 0], rt[:, 4], rt[:, 1], rt[:, 2], rt[:, 3])
            steps += [lambda e: e.tensor_tensor(scale1[:, o], rt[:, 0], rstd[:, o], ALU.mult)]
            t = dchain(steps, [t, last["rt"], *x1_free[o]], "dve_rsqrt")
            x1_ready[b] = last["rt"] = last["mv"] = t
            yield
            for j in range(TPB):
                h_t = dve.run(lambda e, j=j: e.tensor_scalar(h[:, j], xb[:, j], mean1[:, o, j:j + 1], scale1[:, o, j:j + 1], ALU.subtract, ALU.mult),
                              after=[t, last.get("h"), ("pe_pair", 1)], done="dve_h")
            yield
            for c0 in range(0, TPB * KD, 4):
                i, bk, free = misc.take()

                def tr(e, c0=c0, bk=bk):
                    for c in range(4):
                        j, k = c0 // KD + c % 2, c // 2
                        m = e.transpose(bk[:, c * P:(c + 1) * P], h[:, j, k * P:(k + 1) * P], ident)
                    return m
                tt = pe.run(tr, after=[h_t, *free], done="pe_hT")
                hT_t = act.run(lambda e, c0=c0, bk=bk: e.activation(
                    hT[:, :, c0 // KD * P:(c0 // KD + 2) * P], bk.rearrange("p (k t) -> p k t", k=KD), ACT.Copy), after=[tt, last.get("hT")], done="act_hT")
                misc.release(i, hT_t)
                yield
            last["h"] = tt
            i, bk, free = misc.take()

            def vm(e, bk=bk):
                for j in range(TPB):
                    for k in range(KD):
                        m = e.matmul(bk[:, j * NKV * HD:(j + 1) * NKV * HD], hT[:, k, j * P:(j + 1) * P], wqkv_s[:, k, QK:QKV], start=(k == 0), stop=(k == KD - 1))
                return m
            tt = pe.run(vm, after=[hT_t, wq_ready, *free], done="pe_v")
            v_ready[b] = act.run(lambda e, bk=bk: e.activation(
                v1[o][:, :, :, 0:HD], bk.rearrange("p (t g c) -> p t g c", t=TPB, g=NKV), ACT.Copy),
                after=[tt, v_set, *v1_free[o]], done="act_v")
            misc.release(i, v_ready[b])
            yield
            for c in range(QR):
                for r0 in range(0, QK, P):
                    n = min(P, QK - r0)
                    cols = slice(c * CH, (c + 1) * CH)
                    got = []
                    for w in (wqkv_s, wrot_s):
                        i, bk, free = misc.take()

                        def mm(e, w=w, bk=bk, r0=r0, n=n, cols=cols):
                            for k in range(KD):
                                m = e.matmul(bk[0:n, :], w[:, k, r0:r0 + n], hT[:, k, cols], start=(k == 0), stop=(k == KD - 1))
                            return m
                        tt = pe.run(mm, after=[hT_t, wq_ready, *free], done="pe_qk")
                        tab, dst = (cosT, rot1) if w is wqkv_s else (sinT, rot2)
                        t = dve.run(lambda e, bk=bk, tab=tab, dst=dst, n=n, cols=cols: e.tensor_tensor(dst[0:n], bk[0:n, :], tab[0:n, cols], ALU.mult),
                                    after=[tt, last.get("rot"), *rope_t], done="dve_rope")
                        misc.release(i, t)
                        got.append(t)
                    i, sp3, free = splits.take()
                    t = dve.run(lambda e, n=n: e.tensor_tensor(qk32[0:n], rot1[0:n], rot2[0:n], ALU.add), after=[got[1], last.get("qk32")], done="dve_rope")
                    last["rot"] = t
                    th = act.run(lambda e, n=n, s=sp3: e.activation(s[0:n, 0], qk32[0:n], ACT.Copy), after=[t, *free], done="act_split")
                    tr_ = pool.run(lambda e, n=n, s=sp3: e.tensor_tensor(qres[0:n], qk32[0:n], s[0:n, 0], ALU.subtract), after=[th, last.get("qres")], done="pool_split")
                    last["qk32"] = tr_
                    tm = act.run(lambda e, n=n, s=sp3: e.activation(s[0:n, 1], qres[0:n], ACT.Copy), after=[tr_], done="act_split")
                    tl = pool.run(lambda e, n=n, s=sp3: e.tensor_tensor(s[0:n, 2], qres[0:n], s[0:n, 1], ALU.subtract), after=[tm], done="pool_split")
                    last["qres"] = tl
                    ts = split_store.start(lambda e, n=n, s=sp3, r0=r0, cols=cols: e.dma_start(
                        parts[b][:, r0:r0 + n, cols].rearrange("s r t -> r s t"), s[0:n]), after=[tl, tm])
                    splits.release(i, ts)
                    parts_ready.setdefault(b, []).append(ts)
                    yield
            last["hT"] = tt

        stack_ready, stack_free = {}, [(), ()]
        max_ready = {}

        def load_stack(b, g):
            s = stack[(b * NKV + g) % 2]
            free = stack_free[(b * NKV + g) % 2]
            lot = []
            for r, (qp, kp) in enumerate(zip(QPART, KPART)):
                to = slice(r * HD, (r + 1) * HD)
                lot.append(lambda e, to=to, qp=qp: e.dma_start(
                    s[to, 0:GRP, :], parts[b][qp, g * GRP * HD:(g + 1) * GRP * HD, :].rearrange("(h i) t -> i h t", i=HD)))
                lot.append(lambda e, to=to, kp=kp: e.dma_start(
                    s[to, GRP, :], parts[b][kp, (NH + g) * HD:(NH + g + 1) * HD, :]))
            stack_ready[b, g] = [stack_load.start(*lot, after=[*parts_ready[b], *free])]

        def max_pass(b, g, r):
            s = stack[(b * NKV + g) % 2]
            units = []
            for jj in range(TPR):
                j = r * TPR + jj
                if r:
                    units += [(j, 0, CH, [hh], False, 0) for hh in range(GRP)]
                w = (jj + 1) * P
                nh = {1: 4, 2: 2}.get(jj + 1, 1)
                units += [(j, r * CH, w, list(range(h0, h0 + nh)), True, 1 if r else 0) for h0 in range(0, GRP, nh)]
            for j, k0, w, heads, diag, chunk in units:
                i, bk, free = max_banks.take()

                def mm(e, j=j, k0=k0, w=w, heads=heads, diag=diag, bk=bk):
                    for c, hh in enumerate(heads):
                        m = e.matmul(bk[:, c * w:(c + 1) * w], s[0:STACK, hh, j * P:(j + 1) * P], s[0:STACK, GRP, k0:k0 + w], start=True, stop=not diag)
                        if diag:
                            m = e.matmul(bk[:, (c + 1) * w - P:(c + 1) * w], identb, causal, start=False, stop=True)
                    return m
                t = pe.run(mm, after=[*stack_ready[b, g], const_t, *free], done="pe_max")
                to = mx[:, chunk, :].rearrange("p (h j) -> p h j", h=GRP)[:, heads[0]:heads[-1] + 1, j % TPR]
                t = dve.run(lambda e, w=w, n=len(heads), bk=bk, to=to: e.tensor_reduce(
                    to, bk[:, 0:n * w].rearrange("p (h k) -> p h k", h=n), AX.X, ALU.max), after=[t, last.get("mx")], done="dve_max")
                max_banks.release(i, t)
                yield
            if r:
                src = mxc
                t = dve.run(lambda e: e.tensor_tensor(mxc, mx[:, 0], mx[:, 1], ALU.max), after=[t, last.get("mxc")], done="dve_max")
                last["mx"] = t
            else:
                src = mx[:, 0]
            i, bk, free = misc.take()
            tt = pe.run(lambda e, bk=bk: e.transpose(bk[0:16, 0:P], src, ident), after=[t, *free], done="pe_maxT")
            last["mxc" if r else "mx"] = tt
            t1 = dve.run(lambda e, bk=bk: e.tensor_scalar(mneg, bk[0:16, 0:P], -1.0, None, ALU.mult), after=[tt], done="dve_neg")
            misc.release(i, t1)
            t2 = dve.run(lambda e: e.tensor_copy(mneg_parts[:, 0], mneg), after=[t1, *last.get("mneg", ())], done="dve_neg")
            t3 = dve.run(lambda e: e.tensor_tensor(mneg_parts[:, 1], mneg, mneg_parts[:, 0], ALU.subtract), after=[t2], done="dve_neg")
            got = [max_load.start(*[lambda e, c=c, hh=hh: e.dma_start(
                s[STACK + c:STACK + c + 1, hh, r * CH:(r + 1) * CH],
                mneg_parts[hh * TPR:(hh + 1) * TPR, c, :]) for c in range(NMAX) for hh in range(GRP)], after=[t3])]
            last["mneg"] = got
            max_ready[b, g, r] = got
            yield

        pack_ready = {}

        def attend(b, g, r):
            o = b % 2
            s = stack[(b * NKV + g) % 2]
            ipv, pv, pv_free = pv_bank.take()
            nk = (r + 1) * TPR
            held = []

            def pv_mm(kt, ip, pb, q0, ready):
                def mm(e):
                    for hh in range(GRP):
                        m = e.matmul(pv[32 * hh:32 * hh + 32, q0:CH], v1[o][:, kt, g, :], pb[:, hh, q0:CH], start=(kt == 0), stop=(kt == nk - 1))
                    return m
                t = pe.run(mm, after=[*ready, v_ready[b], *(pv_free if kt == 0 else ())], done="pe_pv")
                probs.release(ip, t)
                return t
            for kt in range(nk):
                q0 = max(kt * P - r * CH, 0)
                ip, pb, p_free = probs.take()
                for hh in range(GRP):
                    i, bk, free = score_banks.take()
                    t = pe.run(lambda e, kt=kt, hh=hh, q0=q0, bk=bk: e.matmul(
                        bk[:, q0:CH], s[0:STACK + NMAX, GRP, kt * P:(kt + 1) * P], s[0:STACK + NMAX, hh, r * CH + q0:(r + 1) * CH], start=True, stop=True),
                        after=[*max_ready[b, g, r], ones_set, *free], done="pe_scores")
                    score_t = t
                    t = act.run(lambda e, hh=hh, q0=q0, bk=bk, pb=pb: e.activation(pb[:, hh, q0:CH], bk[:, q0:CH], ACT.Exp, scale=float(HD) ** -0.5),
                                after=[t, *(p_free if hh == 0 else ())], done="act_exp")
                    score_banks.release(i, t)
                    yield
                ready = [t]
                if kt >= r * TPR:
                    t = pool.run(lambda e, q0=q0, pb=pb: e.affine_select(
                        pb[:, :, q0:q0 + P], pb[:, :, q0:q0 + P], [[0, GRP], [1, P]], ALU.is_ge, 0.0, base=0, channel_multiplier=-1),
                        after=[t], done="pool_causal")
                    ready.append(t)
                held.append((kt, ip, pb, q0, ready))
                if len(held) > 1:
                    pv_t = pv_mm(*held.pop(0))
                    yield
            stack_last = score_t
            pv_t = pv_mm(*held.pop(0))
            t1 = act.run(lambda e: e.activation(onorm, pv, ACT.Copy), after=[pv_t, *last.get("onorm", ())], done="act_pv")
            pv_bank.release(ipv, t1)
            t2 = dve.run(lambda e: e.stream_shuffle(osum, onorm, [HD] * 32), after=[t1, const_t], done="dve_norm")
            t3 = dve.run(lambda e: e.reciprocal(osum, osum), after=[t2], done="dve_norm")
            t4 = dve.run(lambda e: e.tensor_tensor(onorm, onorm, osum, ALU.mult), after=[t3], done="dve_norm")
            k, row = divmod(g * GRP * HD, P)
            last["onorm"] = [pack_move.start(*[lambda e, hh=hh: e.dma_start(
                attnT[row + hh * HD:row + (hh + 1) * HD, k, r * CH:(r + 1) * CH], onorm[32 * hh:32 * hh + HD, :]) for hh in range(GRP)],
                after=[t4, *last.get("attnT", ())])]
            pack_ready.setdefault(b, []).extend(last["onorm"])
            if r == QR - 1:
                stack_free[(b * NKV + g) % 2] = (stack_last, ("pe_max", pe.count["pe_max"]))
            yield

        def close(b):
            o = b % 2
            il, lg, l_free = None, None, None
            for j in range(TPB):
                i, bk, free = misc.take()

                def mm(e, j=j, bk=bk):
                    for k in range(KD):
                        m = e.matmul(bk[:, 0:D], attnT[:, k, j * P:(j + 1) * P], wo_s[:, k], start=(k == 0), stop=(k == KD - 1))
                    return m
                tt = pe.run(mm, after=[*pack_ready[b], wo_t, *free], done="pe_wo")
                hr = hrow[:, b * TPB + j, 0:D]
                t1 = dve.run(lambda e, j=j: e.tensor_scalar(yrow, x1[o][:, j], mean1[:, o, j:j + 1], rstd[:, o, j:j + 1], ALU.subtract, ALU.mult), after=[x1_ready[b], last.get("yrow")], done="dve_x2")
                t2 = dve.run(lambda e, bk=bk, hr=hr: e.tensor_tensor(hr, bk[:, 0:D], yrow, ALU.add), after=[tt, t1, ids_set], done="dve_x2")
                last["yrow"] = t2
                misc.release(i, t2)
                dve.run(lambda e, j=j, hr=hr: e.bn_stats(st[:, j], hr), after=[t2, last.get("st")], done="dve_stats")
                t3 = pool.run(lambda e, j=j, hr=hr: e.tensor_tensor(x1[o][:, j], x1[o][:, j], hr, ALU.add), after=[t2], done="pool_base")
                base = base_store.start(lambda e, j=j: e.dma_start(out_t[b * TPB + j], x1[o][:, j]), after=[t3])
                yield
            last["attnT"] = (tt,)
            x1_free[o] = base_store.all_landed()
            v1_free[o] = (("pe_pv", pe.count["pe_pv"]),)
            t = ("dve_stats", dve.count["dve_stats"])
            for j in range(TPB):
                dve.run(lambda e, j=j: e.bn_aggr(mv[:, j], st[:, j]), after=[t, last["mv"]], done="dve_aggr")
            t = ("dve_aggr", dve.count["dve_aggr"])
            last["st"] = t
            steps = [lambda e: e.tensor_tensor(rt[:, 4], mv[:, :, 0], mv[:, :, 0], ALU.mult),
                     lambda e: e.tensor_tensor(rt[:, 4], rt[:, 4], mv[:, :, 1], ALU.add)]
            steps += rsqrt_steps(rstd2, rt[:, 4], rt[:, 1], rt[:, 2], rt[:, 3])
            t = dchain(steps, [t, last["rt"], ("pool_base", pool.count["pool_base"])], "dve_rsqrt")
            last["mv"] = last["rt"] = t
            yield
            for j in range(TPB):
                hr = hrow[:, b * TPB + j, 0:D]
                th = dve.run(lambda e, j=j, hr=hr: e.scalar_tensor_tensor(hr, hr, rstd2[:, j:j + 1], ln2_s, ALU.mult, ALU.mult), after=[t, ln2_t], done="dve_h2")
                i, bk, free = misc.take()

                def tr(e, bk=bk, hr=hr):
                    for k in range(KD):
                        m = e.transpose(bk[:, k * P:(k + 1) * P], hr[:, k * P:(k + 1) * P], ident)
                    return m
                tt = pe.run(tr, after=[th, *free], done="pe_h2T")
                te = act.run(lambda e, bk=bk: e.activation(h2T, bk[:, 0:KD * P].rearrange("p (k t) -> p k t", k=KD), ACT.Copy), after=[tt, last.get("h2T")], done="act_h2T")
                misc.release(i, te)
                i, bk, free = misc.take()

                def mm(e, bk=bk):
                    for k in range(KD):
                        m = e.matmul(bk[:, 0:NE], h2T[:, k], gate_s[:, k], start=(k == 0), stop=(k == KD - 1))
                    return m
                tt = pe.run(mm, after=[te, gate_t, *free], done="pe_gate")
                last["h2T"] = tt
                tl = dve.run(lambda e, bk=bk, j=j: e.tensor_copy(logits[:, b * TPB + j], bk[:, 0:NE]), after=[tt], done="dve_logits")
                misc.release(i, tl)
                yield
            last["logits", b] = tl
            last["h2", b] = th

        block_expert, scattered = {}, {}

        def route(gi, mem, mem_free):
            batches = GROUPS[gi]
            t0, nt, nb = batches[0] * TPB, len(batches) * TPB, n_blocks(batches)
            n8 = nt * NE
            top, idx, e1, e2, pos, tot, run_, wts, wk, small, blk = carve(mem, [8, 8, n8, n8, n8, n8, n8, 4 * nt, 2 * nt, 8 * NE, nb + 1])
            picked = hrow
            lg = logits[:, t0:t0 + nt]
            e1v, e2v, posv, totv, runv = (grid(v, nt) for v in (e1, e2, pos, tot, run_))
            wtv = wts.rearrange("p (a t) -> p a t", a=4)
            l1, l2, q1, q2 = (wtv[:, a] for a in range(4))
            n = "dve_route"
            t = dve.run(lambda e: e.memset(wk, 0.0), after=[last["logits", batches[-1]], *mem_free], done=n)
            for c in range(nt):
                t = dchain([lambda e, c=c: e.max(top, lg[:, c]),
                            lambda e, c=c: e.max_index(idx.bitcast(mybir.dt.uint32), top, lg[:, c]),
                            lambda e, c=c: e.tensor_copy(wtv[:, 0:2, c], top[:, 0:2]),
                            lambda e, c=c: e.tensor_copy(wtv[:, 2:4, c], idx.bitcast(mybir.dt.uint32)[:, 0:2])], [t], n)
                if c % 4 == 3:
                    yield
            iota_e = iota[:, 0:NE].unsqueeze(1).broadcast_to([P, nt, NE])
            d = wk[:, 0:nt]
            t = dchain([lambda e: e.tensor_tensor(e1v, iota_e, q1.unsqueeze(2).broadcast_to([P, nt, NE]), ALU.is_equal),
                        lambda e: e.tensor_tensor(e2v, iota_e, q2.unsqueeze(2).broadcast_to([P, nt, NE]), ALU.is_equal),
                        lambda e: e.tensor_tensor(totv, e1v, e2v, ALU.add),
                        lambda e: e.tensor_copy(run_.bitcast(BF16)[:, 0:n8], tot),
                        lambda e: e.tensor_tensor(d, l2, l1, ALU.subtract)], [t, iota_t], n)
            te = act.run(lambda e: e.activation(d, d, ACT.Exp), after=[t], done="act_route")
            hot = run_.bitcast(BF16)[:, 0:n8]
            i, bk, free = misc.take()

            def mm(e, bk=bk):
                e.matmul(bk[:, 0:n8], before, hot, start=True, stop=True)
                return e.matmul(bk[:, n8:2 * n8], onesb, hot, start=True, stop=True)
            tt = pe.run(mm, after=[t, const_t, *free], done="pe_rank")
            w2c = wk[:, nt:2 * nt]
            cnt, nblk, endb, startb = (small[:, a * NE:(a + 1) * NE] for a in range(4))
            t = dchain([lambda e: e.tensor_scalar(w2c, d, 1.0, None, ALU.add),
                        lambda e: e.reciprocal(l1, w2c),
                        lambda e: e.tensor_tensor(l2, l1, d, ALU.mult),
                        lambda e, bk=bk: e.tensor_copy(pos, bk[:, 0:n8]),
                        lambda e, bk=bk: e.tensor_copy(tot, bk[:, n8:2 * n8])], [te, tt], n)
            misc.release(i, t)
            yield
            ones_nt = onesf[:, 0:nt]
            t = dchain([lambda e, x_=x_: e.tensor_tensor_scan(runv[:, :, x_], ones_nt, totv[:, :, x_], 0.0, ALU.mult, ALU.add) for x_ in range(NE)], [t], n)
            steps = [lambda e: e.tensor_copy(cnt, runv[:, nt - 1]),
                     lambda e: e.tensor_tensor(run_, run_, tot, ALU.subtract),
                     lambda e: e.tensor_tensor(pos, pos, run_, ALU.add)]
            per = nt
            jm = tot[:, 0:per * NE].rearrange("p (e j) -> p e j", e=NE)
            steps += [lambda e: e.tensor_tensor(jm, cnt.unsqueeze(2).broadcast_to([P, NE, per]),
                                                iota128[:, 0:per].unsqueeze(1).broadcast_to([P, NE, per]), ALU.is_gt),
                      lambda e: e.tensor_reduce(nblk, jm, AX.X, ALU.add),
                      lambda e: e.tensor_tensor_scan(endb, onesf[:, 0:NE], nblk, 0.0, ALU.mult, ALU.add),
                      lambda e: e.tensor_tensor(startb, endb, nblk, ALU.subtract),
                      lambda e: e.scalar_tensor_tensor(posv, startb.unsqueeze(1).broadcast_to([P, nt, NE]), float(P), posv, ALU.mult, ALU.add),
                      lambda e: e.tensor_tensor(e1, e1, pos, ALU.mult),
                      lambda e: e.tensor_tensor(e2, e2, pos, ALU.mult),
                      lambda e: e.tensor_reduce(q1, e1v, AX.X, ALU.add),
                      lambda e: e.tensor_reduce(q2, e2v, AX.X, ALU.add),
                      lambda e: e.tensor_copy(d.bitcast(I32), q1),
                      lambda e: e.tensor_copy(w2c.bitcast(I32), q2)]
            t = dchain(steps, [t], n)
            pos_t = t
            yield
            bi = blk[0:1, 0:nb].bitcast(I32)
            acc = blk[0:1, 0:nb]
            steps = [lambda e: e.tensor_scalar(acc, iota[0:1, 0:nb], endb[0:1, 0:1], None, ALU.is_ge)]
            for x_ in range(1, NE - 1):
                steps += [lambda e, x_=x_: e.scalar_tensor_tensor(acc, iota[0:1, 0:nb], endb[0:1, x_:x_ + 1], acc, ALU.is_ge, ALU.add)]
            steps += [lambda e: e.tensor_scalar(bexp[gi], acc, float(2 * FFN), None, ALU.mult)]
            t = dchain(steps, [t], n)
            block_expert[gi] = t
            got = []
            wt_t = None
            for k, (w, at) in enumerate(((l1, d), (l2, w2c))):
                if k:
                    after = [a for a in scatter.all_landed()]
                else:
                    after = []
                wt_t = dve.run(lambda e, w=w: e.tensor_copy(hrow[:, t0:t0 + nt, D + 1], w), after=[pos_t, *after], done="dve_weight")
                for c in range(nt):
                    got.append(scatter.start(lambda e, c=c, at=at: e.indirect_dma_start(
                        rows[gi], bass.IndirectOffsetOnAxis(ap=at.bitcast(I32)[:, c:c + 1], axis=0), hrow[:, t0 + c, :], None),
                        after=[wt_t, pads[gi], last["h2", batches[-1]]]))
                    yield
            scattered[gi] = scatter.all_landed()
            last["routed", gi] = ("dve_route", dve.count["dve_route"])

        def load_w13():
            for k in range(KD):
                for e_ in range(NE):
                    last.setdefault("w13", []).append(weight_load.start(lambda e, k=k, e_=e_: e.dma_start(
                        w13_s[:, k, e_ * 2 * FFN:(e_ + 1) * 2 * FFN], w13T[k * P:(k + 1) * P, e_, :]),
                        after=[last["hT"], ("dve_rope", dve.count["dve_rope"]), ("dve_h", dve.count["dve_h"]), *split_store.all_landed()]))
                    yield

        def load_w2(after):
            for e_ in range(NE):
                last.setdefault("w2", []).append(weight_load.start(lambda e, e_=e_: e.dma_start(
                    w2_mem[:, e_ * KF * D:(e_ + 1) * KF * D].rearrange("p (k n) -> p k n", k=KF), w2T[:, e_, :].rearrange("(k p) n -> p k n", p=P)), after=after))
                yield

        (rb, rhT, rsl, rg, rgT, ry) = carve(stack_mem, [3 * RW, 2 * KD * P, 2 * FFN, 2 * FFN, 2 * FFN, 2 * D])
        blocks = Ring([rb[:, i * RW:(i + 1) * RW] for i in range(3)])
        blockT = Ring([rhT[:, i * KD * P:(i + 1) * KD * P].rearrange("p (k t) -> p k t", k=KD) for i in range(2)])
        silus = Ring([rsl[:, i * FFN:(i + 1) * FFN] for i in range(2)])
        gated = Ring([rg[:, i * FFN:(i + 1) * FFN] for i in range(2)])
        gatedT = Ring([rgT[:, i * FFN:(i + 1) * FFN] for i in range(2)])
        youts = Ring([ry[:, i * D:(i + 1) * D] for i in range(2)])
        up_banks = Ring([(bank[0], bank[1]), (bank[2], bank[3])])
        gT_banks = Ring([bank[4]])
        y_bank = Ring([bank[5]])

        def experts(work):
            first = [*last["att_done"]]
            for rg_ in (up_banks, gT_banks, y_bank, blocks, blockT, silus, gated, gatedT, youts):
                rg_.free = [tuple(first)] * len(rg_.buffers)
            n = len(work)
            got, state = {}, {}

            def fetch(w):
                gi, c = work[w]
                i, buf, free = blocks.take()
                got[w] = (i, buf, block_load.start(lambda e, gi=gi, c=c, buf=buf: e.dma_start(buf, rows[gi][c * P:(c + 1) * P, :]),
                                                  after=[*free, *scattered[gi]]))

            def turn(w):
                i, buf, ready = got[w]
                im, bk, free = misc.take()

                def tr(e):
                    for k in range(KD):
                        m = e.transpose(bk[:, k * P:(k + 1) * P], buf[:, k * P:(k + 1) * P], ident)
                    return m
                tt = pe.run(tr, after=[ready, *free], done="pe_blockT")
                ib, bT, bfree = blockT.take()
                te = dve.run(lambda e: e.tensor_copy(bT, bk[:, 0:KD * P].rearrange("p (k t) -> p k t", k=KD)), after=[tt, *bfree], done="dve_blockT")
                misc.release(im, te)
                state[w] = (ib, bT, te)

            def up(w):
                gi, c = work[w]
                ib, bT, te = state[w]
                iu, (b1, b3), free = up_banks.take()

                def mm(e):
                    v = e.value_load(bexp[gi][0:1, c:c + 1], min_val=0, max_val=(NE - 1) * 2 * FFN)
                    offs[w] = v
                    for half, bk in enumerate((b1, b3)):
                        for k in range(KD):
                            m = e.matmul(bk, bT[:, k], w13_s[:, k, bass.ds(v + half * FFN, FFN)], start=(k == 0), stop=(k == KD - 1))
                    return m
                tt = pe.run(mm, after=[te, block_expert[gi], *last["w13"], *free], done="pe_up")
                blockT.release(ib, tt)
                isl, sl, sfree = silus.take()
                ts = act.run(lambda e: e.activation(sl, b1, ACT.Silu), after=[tt, *sfree], done="act_silu")
                ig, g_, gfree = gated.take()
                tg = dve.run(lambda e: e.tensor_tensor(g_, b3, sl, ALU.mult), after=[ts, *gfree], done="dve_gated")
                silus.release(isl, tg)
                up_banks.release(iu, ts, tg)
                state[w] = (ig, g_, tg)

            def turn_gated(w):
                ig, g_, tg = state[w]
                i, bk, free = gT_banks.take()

                def tr(e):
                    for k in range(KF):
                        m = e.transpose(bk[:, k * P:(k + 1) * P], g_[:, k * P:(k + 1) * P], ident)
                    return m
                tt = pe.run(tr, after=[tg, *free], done="pe_gatedT")
                gated.release(ig, tt)
                it, gT, tfree = gatedT.take()
                te = act.run(lambda e: e.activation(gT, bk, ACT.Copy), after=[tt, *tfree], done="act_gatedT")
                gT_banks.release(i, te)
                state[w] = (it, gT, te)

            def down(w):
                gi, c = work[w]
                it, gT, te = state[w]
                ib, buf, _ = got[w]
                i, bk, free = y_bank.take()

                def mm(e):
                    v = offs[w]
                    for k in range(KF):
                        m = e.matmul(bk[:, 0:D], gT[:, k * P:(k + 1) * P], w2_mem[:, bass.ds(v + k * D, D)], start=(k == 0), stop=(k == KF - 1))
                    return m
                tt = pe.run(mm, after=[te, *last["w2"], *free], done="pe_down")
                gatedT.release(it, tt)
                iy, y, yfree = youts.take()
                ty = dve.run(lambda e: e.tensor_scalar(y, bk[:, 0:D], buf[:, D + 1:D + 2], None, ALU.mult), after=[tt, *yfree], done="dve_y")
                y_bank.release(i, ty)
                ta = add_out.start(lambda e: e.indirect_dma_start(
                    out_rows, bass.IndirectOffsetOnAxis(ap=buf.bitcast(I32)[:, D:D + 1], axis=0), y, None,
                    bounds_check=NBATCH * SEQ - 1, oob_is_err=False, compute_op=ALU.add), after=[ty, *base_store.all_landed()])
                youts.release(iy, ta)
                blocks.release(ib, ta, ty)
            offs = {}
            fetch(0)
            fetch(1)
            turn(0)
            for w in range(n + 1):
                if w < n:
                    up(w)
                if w + 1 < n:
                    turn(w + 1)
                if w >= 1:
                    down(w - 1)
                if w + 2 < n:
                    fetch(w + 2)
                if w < n:
                    turn_gated(w)

        bexp = [sb(f"bexp{i}", [1, n_blocks(g)], I32) for i, g in enumerate(GROUPS)]

        def drain(g):
            for _ in g:
                pass

        def chain(*gs):
            for g in gs:
                yield from g

        turns = [(b, g, r) for b in range(NBATCH) for g in range(NKV) for r in range(QR)]
        drain(project(0))
        load_stack(0, 0)
        drain(max_pass(0, 0, 0))
        side = None
        for n, (b, g, r) in enumerate(turns):
            if (g, r) == (0, 0):
                if b + 1 < NBATCH:
                    side = project(b + 1)
                else:
                    side = chain(route(0, route_a, ()), load_w13(), load_w2(None)) if False else None
            if r == 0 and g + 1 < NKV:
                load_stack(b, g + 1)
            if (g, r) == (NKV - 1, 0) and b + 1 < NBATCH:
                drain(side)
                load_stack(b + 1, 0)
            nxt = max_pass(*turns[n + 1]) if n + 1 < len(turns) else iter(())
            for k, _ in enumerate(attend(b, g, r)):
                next(nxt, None)
                if side is not None and k % 2:
                    next(side, None)
            drain(nxt)
            if (g, r) == (NKV - 1, QR - 1):
                drain(close(b))
                if b == GROUPS[0][-1]:
                    drain(route(0, route_a, ()))
                    last["w2_free"] = [last["routed", 0], *scattered[0], *x1_free[0], *v1_free[0], ("pe_square", pe.count["pe_square"]),
                                       ("pe_qk", pe.count["pe_qk"]), ("pe_v", pe.count["pe_v"])]
                    drain(load_w13())
                    drain(load_w2(last["w2_free"]))
        last["att_done"] = [("pe_pv", pe.count["pe_pv"]), ("act_pv", act.count["act_pv"]), ("dve_max", dve.count["dve_max"]), ("pe_scores", pe.count["pe_scores"]),
                            ("act_exp", act.count["act_exp"]), ("pe_max", pe.count["pe_max"])]
        drain(route(1, probs_mem, last["att_done"]))
        experts([(0, c) for c in range(n_blocks(GROUPS[0]))] + [(1, c) for c in range(n_blocks(GROUPS[1]))])
        pool.wait(*add_out.all_landed())
        sp.wait(*add_out.all_landed(), *base_store.all_landed())

        block = ctx.enter_context(nc.Block())

        @block.sync
        def _(e):
            sp.play(e)

        @block.gpsimd
        def _(e):
            pool.play(e)

        @block.scalar
        def _(e):
            act.play(e)

        @block.vector
        def _(e):
            dve.play(e)

        @block.tensor
        def _(e):
            pe.play(e)


def rope_tables():
    inv_freq = (np.float32(1.0) / np.power(np.float32(THETA), np.arange(0, HD, 2, dtype=np.float32) / np.float32(HD))).astype(np.float32)
    freqs = np.arange(SEQ, dtype=np.float32)[:, None] * inv_freq[None, :]
    cos = np.concatenate([np.cos(freqs)] * 2, axis=1).T
    sin = np.concatenate([-np.sin(freqs), np.sin(freqs)], axis=1).T
    return np.ascontiguousarray(np.tile(cos, (P // HD, 1))), np.ascontiguousarray(np.tile(sin, (P // HD, 1)))


def kernel(L0_attn_x, L0_attn_W_theta, L0_attn_W_phi, L0_attn_W_g, L0_ffn_ln1_w, L0_ffn_ln2_w,
           L0_ffn_wqkv, L0_ffn_wo, L0_ffn_gate_w, L0_ffn_w13, L0_ffn_w2):
    import concourse.bacc as bacc
    from concourse.bass_utils import run_bass_kernel_spmd

    def lay(a):
        return np.ascontiguousarray(np.asarray(a))

    wqkv = np.asarray(L0_ffn_wqkv)
    swap = np.arange(QK).reshape(-1, 2, HD // 2)[:, ::-1].reshape(-1)
    cos, sin = rope_tables()
    tri = np.stack([np.triu(np.ones((P, P), np.float32), 1)] * 2, axis=1)
    ids = np.arange(NTILE * P, dtype=np.int32).reshape(NTILE, P).T
    arrays = {
        "x": lay(L0_attn_x), "wtheta": lay(L0_attn_W_theta), "wphi": lay(L0_attn_W_phi), "wgT": lay(np.asarray(L0_attn_W_g).T),
        "ln1": lay(L0_ffn_ln1_w), "ln2": lay(L0_ffn_ln2_w), "wqkvT": lay(wqkv.T), "wrotT": lay(wqkv[swap].T),
        "woT": lay(np.asarray(L0_ffn_wo).T), "gateT": lay(np.asarray(L0_ffn_gate_w).T),
        "w13T": lay(np.asarray(L0_ffn_w13).transpose(2, 0, 1)), "w2T": lay(np.asarray(L0_ffn_w2).transpose(2, 0, 1)),
        "cos_t": cos, "sin_t": sin, "eye": np.eye(P, dtype=np.float32), "tri": lay(tri), "ids": lay(ids),
    }
    nc = bacc.Bacc("TRN2", target_bir_lowering=False, num_devices=1)
    ins = {f"in_{k}": v for k, v in arrays.items()}
    args = [nc.dram_tensor(k, v.shape, mybir.dt.from_np(v.dtype), kind="ExternalInput").ap() for k, v in ins.items()]
    out = nc.dram_tensor("out_0", [NBATCH, SEQ, D], F32, kind="ExternalOutput").ap()
    mega_kernel(nc, *args, out)
    r = run_bass_kernel_spmd(nc, [ins], core_ids=[0])
    return r.results[0]["out_0"]
```

```python
from contextlib import ExitStack

import numpy as np

import concourse.bass as bass
from concourse import mybir

F32 = mybir.dt.float32
BF16 = mybir.dt.bfloat16
I32 = mybir.dt.int32
ALU = mybir.AluOpType
ACT = mybir.ActivationFunctionType
AX = mybir.AxisListType

P = 128
NBATCH, SEQ, D = 4, 1024, 256
KD = D // P
TPB = SEQ // P
NTILE = NBATCH * TPB
LATENT = 64
NH, NKV, HD = 16, 4, 16
GRP = NH // NKV
QK = (NH + NKV) * HD
QKV = (NH + 2 * NKV) * HD
NE, TOPK, FFN = 8, 2, 512
KF = FFN // P
EPS = 1e-5
CH = 512
QR = SEQ // CH
TPR = CH // P
THETA = 10000.0

QPART = (0, 0, 0, 1, 1, 2)
KPART = (0, 1, 2, 0, 1, 0)
STACK = len(QPART) * HD
NMAX = 2
MASKED = -1e38

GROUPS = ((0, 1, 2), (3,))
RW = D + 2
NOWHERE = 1 << 20


def n_blocks(batches):
    return (TOPK * len(batches) * SEQ + NE * (P - 1)) // P


class Engine:

    def __init__(self, make):
        self.make, self.steps, self.count, self.waited = make, [], {}, {}
        self.latest = None

    def wait(self, *ticks):
        for t in ticks:
            if t is not None and self.waited.get(t[0], 0) < t[1]:
                self.waited[t[0]] = t[1]
                self.steps.append(lambda e, t=t: e.wait_ge(self.make(t[0]), t[1]))

    def run(self, fn, after=(), done=None):
        self.wait(*after)
        if done is None:
            self.steps.append(fn)
            return None
        self.count[done] = self.count.get(done, 0) + 1
        self.steps.append(lambda e: fn(e).then_inc(self.make(done), 1))
        self.latest = (done, self.count[done])
        return self.latest

    def play(self, e):
        for s in self.steps:
            s(e)


class Loads:

    def __init__(self, engine, name, depth):
        self.engine, self.name, self.depth, self.n = engine, name, depth, 0
        self.sent = [0] * depth

    def start(self, *fns, after=()):
        i = self.n % self.depth
        self.n += 1
        sem = f"{self.name}{i}"
        if self.sent[i]:
            self.engine.wait((sem, self.sent[i]))
        self.engine.wait(*after)
        for fn in fns:
            self.engine.steps.append(lambda e, fn=fn: fn(e).then_inc(self.engine.make(sem), 16))
        self.sent[i] += 16 * len(fns)
        return (sem, self.sent[i])

    def all_landed(self):
        return [(f"{self.name}{i}", n) for i, n in enumerate(self.sent) if n]


class Ring:

    def __init__(self, buffers):
        self.buffers, self.n = buffers, 0
        self.free = [()] * len(buffers)

    def take(self):
        i = self.n % len(self.buffers)
        self.n += 1
        return i, self.buffers[i], self.free[i]

    def release(self, i, *ticks):
        self.free[i] = ticks


def mega_kernel(nc, x, wtheta, wphi, wgT, ln1, ln2, wqkvT, wrotT, woT, gateT, w13T, w2T,
                cos_t, sin_t, eye, tri, ids, out):
    with ExitStack() as ctx:
        sems = {}

        def make(name):
            if name not in sems:
                sems[name] = ctx.enter_context(nc.semaphore(name))
            return sems[name]

        def sb(name, shape, dt=F32):
            return ctx.enter_context(nc.sbuf_tensor(name, shape, dt))[:]

        pe, act, dve, pool, sp = (Engine(make) for _ in range(5))
        load = Loads(sp, "load", 8)
        split_store = Loads(sp, "split_store", 4)
        stack_load = Loads(sp, "stack_load", 3)
        max_load = Loads(sp, "max_load", 2)
        pack_move = Loads(sp, "pack_move", 3)
        sum_move = Loads(sp, "sum_move", 4)
        base_store = Loads(sp, "base_store", 4)
        weight_load = Loads(sp, "weight_load", 4)
        block_load = Loads(sp, "block_load", 6)
        pad_store = Loads(sp, "pad_store", 2)
        scatter = Loads(pool, "scatter", 6)
        add_out = Loads(pool, "add_out", 1)

        w13_mem = sb("w13_mem", [P, KD * NE * 2 * FFN])
        w2_mem = sb("w2_mem", [P, NE * KF * D])

        def carve(mem, sizes):
            at, views = 0, []
            for n in sizes:
                views.append(mem[:, at:at + n])
                at += n
            assert at <= mem.shape[1], (at, mem.shape)
            return views

        def grid(view, a):
            return view.rearrange("p (a b) -> p a b", a=a)

        (xn_f, xnT_f, h_f, hT_f, gram_f, gw_f, mix_f, cosT, sinT, rot1, rot2, qk32, qres, split_f) = carve(
            w13_mem, [TPB * D, KD * SEQ, TPB * D, KD * SEQ, KD * D, KD * D, KD * D, SEQ, SEQ, CH, CH, CH, CH, 2 * 3 * CH // 2])
        xn, xnT, h, hT = grid(xn_f, TPB), grid(xnT_f, KD), grid(h_f, TPB), grid(hT_f, KD)
        gram, gw, mix = grid(gram_f, KD), grid(gw_f, KD), grid(mix_f, KD)
        splits = Ring([s.rearrange("p (s q) -> p s q", s=3) for s in (
            split_f.bitcast(BF16)[:, 0:3 * CH], split_f.bitcast(BF16)[:, 3 * CH:6 * CH])])
        (wgT_f, pair_f, wqkv_f, wrot_f, x_even, v_even, route_a) = carve(
            w2_mem, [KD * D, KD * D, KD * QKV, KD * QK, TPB * D, TPB * NKV * 32, 1700])
        wgT_s, pairT, wqkv_s, wrot_s = grid(wgT_f, KD), grid(pair_f, KD), grid(wqkv_f, KD), grid(wrot_f, KD)
        x1 = [grid(x_even, TPB), grid(sb("x_odd", [P, TPB * D]), TPB)]
        v1_flat = [v_even, sb("v_odd", [P, TPB * NKV * 32])]
        v1 = [v.rearrange("p (t g c) -> p t g c", t=TPB, g=NKV) for v in v1_flat]

        w13_s = w13_mem.rearrange("p (k n) -> p k n", k=KD)
        NSTACK, stack_n = 3, (GRP + 1) * SEQ
        stack_mem = sb("stack_mem", [P, NSTACK * stack_n // 2])
        stack = [stack_mem.bitcast(BF16)[:, i * stack_n:(i + 1) * stack_n].rearrange("p (h t) -> p h t", h=GRP + 1)
                 for i in range(NSTACK)]
        probs_mem = sb("probs_mem", [P, 2 * GRP * CH])
        probs = Ring([p.rearrange("p (h q) -> p h q", h=GRP) for p in (probs_mem[:, 0:GRP * CH], probs_mem[:, GRP * CH:])])
        NROW = max(len(g) for g in GROUPS) * TPB
        hrow = sb("hrow", [P, NROW * RW]).rearrange("p (t c) -> p t c", t=NROW)
        attnT = sb("attnT", [P, KD * SEQ]).rearrange("p (k t) -> p k t", k=KD)
        heads_out = Ring([sb("heads_out0", [P, CH]), sb("heads_out1", [P, CH])])
        recip_rows = sb("recip_rows", [P, CH])
        sums = Ring([sb("sums0", [P, GRP * CH // P]), sb("sums1", [P, GRP * CH // P])])
        yrow = sb("yrow", [P, D])
        wo_s = sb("wo_s", [P, KD * D]).rearrange("p (k n) -> p k n", k=KD)
        gate_s = sb("gate_s", [P, KD * NE]).rearrange("p (k n) -> p k n", k=KD)
        ln1_s = sb("ln1_s", [P, KD])
        ln2_s = sb("ln2_s", [P, D])
        ident = sb("ident", [P, P])
        identb = sb("identb", [P, P], BF16)
        causal = sb("causal", [P, P], BF16)
        before = sb("before", [P, P], BF16)
        onesb = sb("onesb", [P, P], BF16)
        st = sb("st", [P, TPB * 6]).rearrange("p (t c) -> p t c", t=TPB)
        mv = sb("mv", [P, TPB * 2]).rearrange("p (t c) -> p t c", t=TPB)
        rt = sb("rt", [P, 6 * TPB]).rearrange("p (a t) -> p a t", a=6)
        rstd, mean1, scale1 = (sb(n, [P, 2 * TPB]).rearrange("p (b t) -> p b t", b=2) for n in ("rstd", "mean1", "scale1"))
        rstd2 = sb("rstd2", [P, TPB])
        mx = sb("mx", [P, 2 * 16]).rearrange("p (c n) -> p c n", c=2)
        mxc = sb("mxc", [P, 16])
        mneg = sb("mneg", [16, P])
        mneg_parts = sb("mneg_parts", [16, NMAX * P], BF16).rearrange("p (s q) -> p s q", s=NMAX)
        h2T = sb("h2T", [P, KD * P]).rearrange("p (k t) -> p k t", k=KD)
        logits = sb("logits", [P, NTILE * NE]).rearrange("p (t e) -> p t e", t=NTILE)
        ids_s = sb("ids_s", [P, NTILE], I32)

        bank = [ctx.enter_context(nc.psum_tensor(f"bank{i}", [P, CH], F32))[:] for i in range(8)]
        max_banks = Ring([bank[0], bank[1]])
        score_banks = Ring([bank[2], bank[3], bank[4]])
        pv_bank = Ring([bank[5]])
        misc = Ring([bank[6], bank[7]])

        recips = nc.dram_tensor("recips", [NBATCH * NKV * QR, GRP, CH], F32, kind="Internal").ap()
        parts = [nc.dram_tensor(f"qk_parts{b}", [3, QK, SEQ], BF16, kind="Internal").ap() for b in range(NBATCH)]
        rows = [nc.dram_tensor(f"routed{i}", [n_blocks(g) * P, RW], F32, kind="Internal").ap() for i, g in enumerate(GROUPS)]
        x_v = x.rearrange("b (j p) d -> b p j d", p=P)
        out_t = out.rearrange("b (j p) d -> (b j) p d", p=P)
        out_rows = out.rearrange("b n d -> (b n) d")

        def kview(w):
            return w.rearrange("(k p) n -> p k n", p=P)

        x_tick = {0: load.start(lambda e: e.dma_start(x1[0], x_v[0]))}
        eye_t = load.start(lambda e: e.dma_start(ident, eye))
        wt_f, wp_f = h_f[0:LATENT, 0:D], h_f[0:LATENT, D:2 * D]
        tp_t = [load.start(lambda e: e.dma_start(wt_f, wtheta)), load.start(lambda e: e.dma_start(wp_f, wphi))]
        wg_t = load.start(lambda e: e.dma_start(wgT_s, kview(wgT)))
        wqkv_t = [load.start(lambda e: e.dma_start(wqkv_s, kview(wqkvT))),
                  load.start(lambda e: e.dma_start(wrot_s, kview(wrotT))),
                  load.start(lambda e: e.dma_start(ln1_s, ln1.rearrange("(k p) -> p k", p=P), allow_slow_non_contiguous=True))]
        rope_t = [load.start(lambda e: e.dma_start(cosT, cos_t)), load.start(lambda e: e.dma_start(sinT, sin_t))]
        tri_in = recip_rows[:, 0:2 * P]
        tri_t = load.start(lambda e: e.dma_start(tri_in.rearrange("p (a b) -> p a b", a=2), tri))
        ids_t = load.start(lambda e: e.dma_start(ids_s, ids))
        ln2_t = load.start(lambda e: e.dma_start(ln2_s, ln2.partition_broadcast(P)))
        wo_t = load.start(lambda e: e.dma_start(wo_s, kview(woT)))
        gate_t = load.start(lambda e: e.dma_start(gate_s, kview(gateT)))
        x_tick[1] = load.start(lambda e: e.dma_start(x1[1], x_v[1]))

        def pool_set(fn, after=()):
            n = pool.count.get("pool_set", 0)
            return pool.run(fn, after=[*after, ("pool_set", n)], done="pool_set")

        pad = xnT_f[:, 0:RW]
        pool_set(lambda e: e.memset(pad, 0.0))
        pad_set = pool_set(lambda e: e.memset(pad.bitcast(I32)[:, D:D + 1], NOWHERE))
        for v in v1_flat:
            pool_set(lambda e, v=v: e.memset(v, 0.0))
        for v in v1:
            v_set = pool_set(lambda e, v=v: e.memset(v[:, :, :, HD:HD + 1], 1.0))
        for s in stack:
            ones_set = pool_set(lambda e, s=s: e.memset(s[STACK:STACK + NMAX, GRP, :], 1.0))
        pads = [pad_store.start(lambda e, r=r: e.dma_start(
            r.rearrange("(n p) c -> p n c", p=P), pad.unsqueeze(1).broadcast_to([P, r.shape[0] // P, RW])), after=[pad_set]) for r in rows]
        hrow_i = hrow.bitcast(I32)
        ids_set = pool_set(lambda e: e.tensor_copy(hrow_i[:, :, D], ids_s[:, 0:NROW]), after=[ids_t])
        iota = sb("iota", [P, 96])
        iota128 = sb("iota128", [P, NTILE])
        onesf = sb("onesf", [P, NTILE])
        pool_set(lambda e: e.iota(iota, pattern=[[1, 96]], base=0, channel_multiplier=0, allow_small_or_imprecise_dtypes=True))
        pool_set(lambda e: e.iota(iota128, pattern=[[P, NTILE]], base=0, channel_multiplier=0, allow_small_or_imprecise_dtypes=True))
        iota_t = pool_set(lambda e: e.memset(onesf, 1.0))

        dve.run(lambda e: e.tensor_copy(identb, ident), after=[eye_t], done="dve_const")
        dve.run(lambda e: e.tensor_scalar(causal, tri_in[:, 0:P], MASKED, None, ALU.mult), after=[tri_t], done="dve_const")
        dve.run(lambda e: e.tensor_copy(before, tri_in[:, P:2 * P]), done="dve_const")
        const_t = dve.run(lambda e: e.memset(onesb, 1.0), done="dve_const")
        for k in range(KD):
            dve.run(lambda e, k=k: e.tensor_scalar(wqkv_s[:, k], wqkv_s[:, k], ln1_s[:, k:k + 1], None, ALU.mult), after=wqkv_t, done="dve_wqkv")
            wq_ready = dve.run(lambda e, k=k: e.tensor_scalar(wrot_s[:, k], wrot_s[:, k], ln1_s[:, k:k + 1], None, ALU.mult), done="dve_wqkv")

        i, bk, free = misc.take()

        def pair_mm(e, bk=bk):
            for k in range(KD):
                m = e.matmul(bk[:, k * D:(k + 1) * D], wp_f[:, k * P:(k + 1) * P], wt_f, start=True, stop=True)
            return m
        t = pe.run(pair_mm, after=tp_t, done="pe_pair")
        pair_ready = act.run(lambda e, bk=bk: e.activation(pairT, grid(bk, KD), ACT.Copy, scale=float(D) ** -0.5), after=[t], done="act_pair")
        misc.release(i, pair_ready)

        def dchain(fns, after, name):
            t = None
            for f in fns:
                t = dve.run(f, after=[*after, t] if t else after, done=name)
            return t

        def rsqrt_steps(dst, var, a, u, w):
            ai, ui, di = a.bitcast(I32), u.bitcast(I32), dst.bitcast(I32)
            steps = [lambda e: e.tensor_scalar(a, var, EPS, None, ALU.add),
                     lambda e: e.tensor_scalar(ui, ai, 1, None, ALU.logical_shift_right),
                     lambda e: e.tensor_scalar(di, ui, -1.0, float(0x5F3759DF), ALU.mult, ALU.add)]
            for _ in range(3):
                steps += [lambda e: e.scalar_tensor_tensor(u, dst, -0.5, a, ALU.mult, ALU.mult),
                          lambda e: e.tensor_tensor(w, u, dst, ALU.mult),
                          lambda e: e.scalar_tensor_tensor(dst, w, 1.5, dst, ALU.add, ALU.mult)]
            return steps

        x1_free = [(), ()]
        v1_free = [(), ()]
        x1_ready, v_ready, parts_ready = {}, {}, {}
        last = {}

        def project(b):
            o = b % 2
            xb = x1[o]
            if b not in x_tick:
                x_tick[b] = load.start(lambda e: e.dma_start(xb, x_v[b]), after=x1_free[o])
            for j in range(TPB):
                dve.run(lambda e, j=j: e.bn_stats(st[:, j], xb[:, j]), after=[x_tick[b], last.get("st")], done="dve_stats")
            yield
            t = ("dve_stats", dve.count["dve_stats"])
            for j in range(TPB):
                dve.run(lambda e, j=j: e.bn_aggr(mv[:, j], st[:, j]), after=[t, last.get("mv")], done="dve_aggr")
            t = last["st"] = ("dve_aggr", dve.count["dve_aggr"])
            t = dchain(rsqrt_steps(rt[:, 0], mv[:, :, 1], rt[:, 1], rt[:, 2], rt[:, 3]), [t, last.get("rt")], "dve_rsqrt")
            yield
            for j in range(TPB):
                xn_t = dve.run(lambda e, j=j: e.tensor_scalar(xn[:, j], xb[:, j], mv[:, j, 0:1], rt[:, 0, j:j + 1], ALU.subtract, ALU.mult),
                               after=[t, last.get("xn")], done="dve_xn")
            last["mv"] = last["rt"] = xn_t
            yield
            i, bk, free = misc.take()
            for k in range(KD):
                def gm(e, k=k, bk=bk):
                    for j in range(TPB):
                        m = e.matmul(bk[:, k * D:(k + 1) * D], xn[:, j, k * P:(k + 1) * P], xn[:, j], start=(j == 0), stop=(j == TPB - 1))
                    return m
                t = pe.run(gm, after=[xn_t, *free], done="pe_gram")
                yield
            gram_t = act.run(lambda e, bk=bk: e.activation(gram, grid(bk, KD), ACT.Copy), after=[t], done="act_gram")
            misc.release(i, gram_t)
            for c0 in range(0, TPB * KD, 4):
                i, bk, free = misc.take()

                def tr(e, c0=c0, bk=bk):
                    for c in range(4):
                        j, k = c0 // KD + c % 2, c // 2
                        m = e.transpose(bk[:, c * P:(c + 1) * P], xn[:, j, k * P:(k + 1) * P], ident)
                    return m
                tt = pe.run(tr, after=[xn_t, *free, eye_t, last.get("xnT")], done="pe_xnT")
                xnT_t = act.run(lambda e, c0=c0, bk=bk: e.activation(
                    xnT[:, :, c0 // KD * P:(c0 // KD + 2) * P], bk.rearrange("p (k t) -> p k t", k=KD), ACT.Copy), after=[tt, pads[0], pads[1]], done="act_xnT")
                misc.release(i, xnT_t)
                yield
            last["xn"] = tt

            def square(lhs, rhs, dst, after, name):
                i, bk, free = misc.take()

                def mm(e, bk=bk):
                    for r in range(KD):
                        for k in range(KD):
                            m = e.matmul(bk[:, r * D:(r + 1) * D], lhs[:, k, r * P:(r + 1) * P], rhs[:, k], start=(k == 0), stop=(k == KD - 1))
                    return m
                t = pe.run(mm, after=[*after, *free], done="pe_square")
                t = act.run(lambda e, bk=bk: e.activation(dst, grid(bk, KD), ACT.Copy), after=[t], done="act_square")
                misc.release(i, t)
                return t
            t = square(gram, wgT_s, gw, [gram_t, wg_t], "gw")
            yield
            mix_t = square(pairT, gw, mix, [t, pair_ready], "mix")
            yield
            for j0 in range(0, TPB, 2):
                i, bk, free = misc.take()

                def mm(e, j0=j0, bk=bk):
                    for c in range(2):
                        for k in range(KD):
                            m = e.matmul(bk[:, c * D:(c + 1) * D], xnT[:, k, (j0 + c) * P:(j0 + c + 1) * P], mix[:, k], start=(k == 0), stop=(k == KD - 1))
                    return m
                tt = pe.run(mm, after=[mix_t, xnT_t, *free], done="pe_x1")
                x1_t = dve.run(lambda e, j0=j0, bk=bk: e.tensor_tensor(xb[:, j0:j0 + 2], grid(bk, 2), xb[:, j0:j0 + 2], ALU.add), after=[tt], done="dve_x1")
                misc.release(i, x1_t)
                for j in (j0, j0 + 1):
                    dve.run(lambda e, j=j: e.bn_stats(st[:, j], xb[:, j]), after=[x1_t, last["st"]], done="dve_stats")
                yield
            last["xnT"] = tt
            t = ("dve_stats", dve.count["dve_stats"])
            for j in range(TPB):
                dve.run(lambda e, j=j: e.bn_aggr(mv[:, j], st[:, j]), after=[t, last["mv"]], done="dve_aggr")
            t = ("dve_aggr", dve.count["dve_aggr"])
            last["st"] = t
            steps = rsqrt_steps(rstd[:, o], mv[:, :, 1], rt[:, 1], rt[:, 2], rt[:, 3])
            steps += [lambda e: e.tensor_copy(mean1[:, o], mv[:, :, 0]),
                      lambda e: e.tensor_tensor(rt[:, 4], rstd[:, o], rstd[:, o], ALU.mult),
                      lambda e: e.tensor_tensor(rt[:, 4], rt[:, 4], mv[:, :, 1], ALU.mult)]
            steps += rsqrt_steps(rt[:, 0], rt[:, 4], rt[:, 1], rt[:, 2], rt[:, 3])
            steps += [lambda e: e.tensor_tensor(scale1[:, o], rt[:, 0], rstd[:, o], ALU.mult)]
            t = dchain(steps, [t, last["rt"], *x1_free[o]], "dve_rsqrt")
            x1_ready[b] = last["rt"] = last["mv"] = t
            yield
            for j in range(TPB):
                h_t = dve.run(lambda e, j=j: e.tensor_scalar(h[:, j], xb[:, j], mean1[:, o, j:j + 1], scale1[:, o, j:j + 1], ALU.subtract, ALU.mult),
                              after=[t, last.get("h"), ("pe_pair", 1)], done="dve_h")
            yield
            for c0 in range(0, TPB * KD, 4):
                i, bk, free = misc.take()

                def tr(e, c0=c0, bk=bk):
                    for c in range(4):
                        j, k = c0 // KD + c % 2, c // 2
                        m = e.transpose(bk[:, c * P:(c + 1) * P], h[:, j, k * P:(k + 1) * P], ident)
                    return m
                tt = pe.run(tr, after=[h_t, *free], done="pe_hT")
                hT_t = act.run(lambda e, c0=c0, bk=bk: e.activation(
                    hT[:, :, c0 // KD * P:(c0 // KD + 2) * P], bk.rearrange("p (k t) -> p k t", k=KD), ACT.Copy), after=[tt, last.get("hT")], done="act_hT")
                misc.release(i, hT_t)
                yield
            last["h"] = tt
            i, bk, free = misc.take()

            def vm(e, bk=bk):
                for j in range(TPB):
                    for k in range(KD):
                        m = e.matmul(bk[:, j * NKV * HD:(j + 1) * NKV * HD], hT[:, k, j * P:(j + 1) * P], wqkv_s[:, k, QK:QKV], start=(k == 0), stop=(k == KD - 1))
                return m
            tt = pe.run(vm, after=[hT_t, wq_ready, *free], done="pe_v")
            v_ready[b] = act.run(lambda e, bk=bk: e.activation(
                v1[o][:, :, :, 0:HD], bk.rearrange("p (t g c) -> p t g c", t=TPB, g=NKV), ACT.Copy),
                after=[tt, v_set, *v1_free[o]], done="act_v")
            misc.release(i, v_ready[b])
            yield
            for c in range(QR):
                for r0 in range(0, QK, P):
                    n = min(P, QK - r0)
                    cols = slice(c * CH, (c + 1) * CH)
                    got = []
                    for w in (wqkv_s, wrot_s):
                        i, bk, free = misc.take()

                        def mm(e, w=w, bk=bk, r0=r0, n=n, cols=cols):
                            for k in range(KD):
                                m = e.matmul(bk[0:n, :], w[:, k, r0:r0 + n], hT[:, k, cols], start=(k == 0), stop=(k == KD - 1))
                            return m
                        tt = pe.run(mm, after=[hT_t, wq_ready, *free], done="pe_qk")
                        tab, dst = (cosT, rot1) if w is wqkv_s else (sinT, rot2)
                        t = dve.run(lambda e, bk=bk, tab=tab, dst=dst, n=n, cols=cols: e.tensor_tensor(dst[0:n], bk[0:n, :], tab[0:n, cols], ALU.mult),
                                    after=[tt, last.get("rot"), *rope_t], done="dve_rope")
                        misc.release(i, t)
                        got.append(t)
                    i, sp3, free = splits.take()
                    t = dve.run(lambda e, n=n: e.tensor_tensor(qk32[0:n], rot1[0:n], rot2[0:n], ALU.add), after=[got[1], last.get("qk32")], done="dve_rope")
                    last["rot"] = t
                    th = act.run(lambda e, n=n, s=sp3: e.activation(s[0:n, 0], qk32[0:n], ACT.Copy), after=[t, *free], done="act_split")
                    tr_ = pool.run(lambda e, n=n, s=sp3: e.tensor_tensor(qres[0:n], qk32[0:n], s[0:n, 0], ALU.subtract), after=[th, last.get("qres")], done="pool_split")
                    last["qk32"] = tr_
                    tm = act.run(lambda e, n=n, s=sp3: e.activation(s[0:n, 1], qres[0:n], ACT.Copy), after=[tr_], done="act_split")
                    tl = pool.run(lambda e, n=n, s=sp3: e.tensor_tensor(s[0:n, 2], qres[0:n], s[0:n, 1], ALU.subtract), after=[tm], done="pool_split")
                    last["qres"] = tl
                    ts = split_store.start(lambda e, n=n, s=sp3, r0=r0, cols=cols: e.dma_start(
                        parts[b][:, r0:r0 + n, cols].rearrange("s r t -> r s t"), s[0:n]), after=[tl, tm])
                    splits.release(i, ts)
                    parts_ready.setdefault(b, []).append(ts)
                    yield
            last["hT"] = tt

        stack_ready, stack_free = {}, [()] * NSTACK
        max_ready = {}

        def load_stack(b, g):
            s = stack[(b * NKV + g) % NSTACK]
            free = stack_free[(b * NKV + g) % NSTACK]
            lot = []
            for r, (qp, kp) in enumerate(zip(QPART, KPART)):
                to = slice(r * HD, (r + 1) * HD)
                lot.append(lambda e, to=to, qp=qp: e.dma_start(
                    s[to, 0:GRP, :], parts[b][qp, g * GRP * HD:(g + 1) * GRP * HD, :].rearrange("(h i) t -> i h t", i=HD)))
                lot.append(lambda e, to=to, kp=kp: e.dma_start(
                    s[to, GRP, :], parts[b][kp, (NH + g) * HD:(NH + g + 1) * HD, :]))
            stack_ready[b, g] = [stack_load.start(*lot, after=[*parts_ready[b], *free])]

        def max_pass(b, g, r):
            s = stack[(b * NKV + g) % NSTACK]
            units = []
            for jj in range(TPR):
                j = r * TPR + jj
                if r:
                    units += [(j, 0, CH, [hh], False, 0) for hh in range(GRP)]
                w = (jj + 1) * P
                nh = {1: 4, 2: 2}.get(jj + 1, 1)
                units += [(j, r * CH, w, list(range(h0, h0 + nh)), True, 1 if r else 0) for h0 in range(0, GRP, nh)]
            for j, k0, w, heads, diag, chunk in units:
                i, bk, free = max_banks.take()

                def mm(e, j=j, k0=k0, w=w, heads=heads, diag=diag, bk=bk):
                    for c, hh in enumerate(heads):
                        m = e.matmul(bk[:, c * w:(c + 1) * w], s[0:STACK, hh, j * P:(j + 1) * P], s[0:STACK, GRP, k0:k0 + w], start=True, stop=not diag)
                        if diag:
                            m = e.matmul(bk[:, (c + 1) * w - P:(c + 1) * w], identb, causal, start=False, stop=True)
                    return m
                t = pe.run(mm, after=[*stack_ready[b, g], const_t, *free], done="pe_max")
                to = mx[:, chunk, :].rearrange("p (h j) -> p h j", h=GRP)[:, heads[0]:heads[-1] + 1, j % TPR]
                t = dve.run(lambda e, w=w, n=len(heads), bk=bk, to=to: e.tensor_reduce(
                    to, bk[:, 0:n * w].rearrange("p (h k) -> p h k", h=n), AX.X, ALU.max), after=[t, last.get("mx")], done="dve_max")
                max_banks.release(i, t)
                yield
            if r:
                src = mxc
                t = dve.run(lambda e: e.tensor_tensor(mxc, mx[:, 0], mx[:, 1], ALU.max), after=[t, last.get("mxc")], done="dve_max")
                last["mx"] = t
            else:
                src = mx[:, 0]
            i, bk, free = misc.take()
            tt = pe.run(lambda e, bk=bk: e.transpose(bk[0:16, 0:P], src, ident), after=[t, *free], done="pe_maxT")
            last["mxc" if r else "mx"] = tt
            t1 = dve.run(lambda e, bk=bk: e.tensor_scalar(mneg, bk[0:16, 0:P], -1.0, None, ALU.mult), after=[tt], done="dve_neg")
            misc.release(i, t1)
            t2 = dve.run(lambda e: e.tensor_copy(mneg_parts[:, 0], mneg), after=[t1, *last.get("mneg", ())], done="dve_neg")
            t3 = dve.run(lambda e: e.tensor_tensor(mneg_parts[:, 1], mneg, mneg_parts[:, 0], ALU.subtract), after=[t2], done="dve_neg")
            got = [max_load.start(*[lambda e, c=c, hh=hh: e.dma_start(
                s[STACK + c:STACK + c + 1, hh, r * CH:(r + 1) * CH],
                mneg_parts[hh * TPR:(hh + 1) * TPR, c, :]) for c in range(NMAX) for hh in range(GRP)], after=[t3])]
            last["mneg"] = got
            max_ready[b, g, r] = got
            yield

        pack_ready = {}
        norms = []
        def attend(b, g, r):
            o = b % 2
            s = stack[(b * NKV + g) % NSTACK]
            ipv, pv, pv_free = pv_bank.take()
            nk = (r + 1) * TPR
            held = []

            def pv_mm(kt, ip, pb, q0, ready):
                def mm(e):
                    for hh in range(GRP):
                        m = e.matmul(pv[32 * hh:32 * hh + 32, q0:CH], v1[o][:, kt, g, :], pb[:, hh, q0:CH], start=(kt == 0), stop=(kt == nk - 1))
                    return m
                t = pe.run(mm, after=[*ready, v_ready[b], *(pv_free if kt == 0 else ())], done="pe_pv")
                probs.release(ip, t)
                return t
            for kt in range(nk):
                q0 = max(kt * P - r * CH, 0)
                ip, pb, p_free = probs.take()
                for hh in range(GRP):
                    i, bk, free = score_banks.take()
                    t = pe.run(lambda e, kt=kt, hh=hh, q0=q0, bk=bk: e.matmul(
                        bk[:, q0:CH], s[0:STACK + NMAX, GRP, kt * P:(kt + 1) * P], s[0:STACK + NMAX, hh, r * CH + q0:(r + 1) * CH], start=True, stop=True),
                        after=[*max_ready[b, g, r], ones_set, *free], done="pe_scores")
                    score_t = t
                    t = act.run(lambda e, hh=hh, q0=q0, bk=bk, pb=pb: e.activation(pb[:, hh, q0:CH], bk[:, q0:CH], ACT.Exp, scale=float(HD) ** -0.5),
                                after=[t, *(p_free if hh == 0 else ())], done="act_exp")
                    score_banks.release(i, t)
                    yield
                ready = [t]
                if kt >= r * TPR:
                    t = pool.run(lambda e, q0=q0, pb=pb: e.affine_select(
                        pb[:, :, q0:q0 + P], pb[:, :, q0:q0 + P], [[0, GRP], [1, P]], ALU.is_ge, 0.0, base=0, channel_multiplier=-1),
                        after=[t], done="pool_causal")
                    ready.append(t)
                held.append((kt, ip, pb, q0, ready))
                if len(held) > 1:
                    pv_t = pv_mm(*held.pop(0))
                    yield
            stack_last = score_t
            pv_t = pv_mm(*held.pop(0))
            i, ho, free = heads_out.take()
            t = act.run(lambda e, ho=ho: e.activation(ho, pv, ACT.Copy), after=[pv_t, *free], done="act_pv")
            pv_bank.release(ipv, t)
            norms.append(normalise(b, g, r, i, ho, t))
            if r == QR - 1:
                stack_free[(b * NKV + g) % NSTACK] = (stack_last, ("pe_max", pe.count["pe_max"]))
            yield

        def normalise(b, g, r, i, ho, ho_t):
            n = (b * NKV + g) * QR + r
            isum, sm, free = sums.take()
            t = sum_move.start(lambda e: e.dma_start(sm, ho[HD:P:32, :]), after=[ho_t, *free])
            for _ in range(8):
                yield
            t = dve.run(lambda e: e.reciprocal(sm, sm), after=[t], done="dve_recip")
            t = sum_move.start(lambda e: e.dma_start(recips[n].rearrange("h (p c) -> (h p) c", c=sm.shape[1]), sm), after=[t])
            sums.release(isum, t)
            t = sum_move.start(lambda e: e.dma_start(recip_rows, recips[n].unsqueeze(1).broadcast_to([GRP, 32, CH])), after=[t, const_t, last.get("recip_rows")])
            for _ in range(12):
                yield
            t = last["recip_rows"] = dve.run(lambda e: e.tensor_tensor(ho, ho, recip_rows, ALU.mult), after=[t], done="dve_norm")
            k, row = divmod(g * GRP * HD, P)
            t = pack_move.start(*[lambda e, hh=hh: e.dma_start(
                attnT[row + hh * HD:row + (hh + 1) * HD, k, r * CH:(r + 1) * CH], ho[32 * hh:32 * hh + HD, :]) for hh in range(GRP)],
                after=[t, *last.get("attnT", ())])
            heads_out.release(i, t)
            pack_ready.setdefault(b, []).append(t)
            yield

        def close(b):
            o = b % 2
            first, rows_free = ids_set, []
            if b == GROUPS[1][0]:
                rows_free = scattered[0]
                first = pool_set(lambda e: e.tensor_copy(hrow_i[:, 0:NTILE - NROW, D], ids_s[:, NROW:NTILE]), after=rows_free)
            for j in range(TPB):
                i, bk, free = misc.take()

                def mm(e, j=j, bk=bk):
                    for k in range(KD):
                        m = e.matmul(bk[:, 0:D], attnT[:, k, j * P:(j + 1) * P], wo_s[:, k], start=(k == 0), stop=(k == KD - 1))
                    return m
                tt = pe.run(mm, after=[*pack_ready[b], wo_t, *free], done="pe_wo")
                hr = hrow[:, (b * TPB + j) % NROW, 0:D]
                t1 = dve.run(lambda e, j=j: e.tensor_scalar(yrow, x1[o][:, j], mean1[:, o, j:j + 1], rstd[:, o, j:j + 1], ALU.subtract, ALU.mult), after=[x1_ready[b], last.get("yrow")], done="dve_x2")
                t2 = dve.run(lambda e, bk=bk, hr=hr: e.tensor_tensor(hr, bk[:, 0:D], yrow, ALU.add), after=[tt, t1, first, *rows_free], done="dve_x2")
                last["yrow"] = t2
                misc.release(i, t2)
                dve.run(lambda e, j=j, hr=hr: e.bn_stats(st[:, j], hr), after=[t2, last.get("st")], done="dve_stats")
                t3 = pool.run(lambda e, j=j, hr=hr: e.tensor_tensor(x1[o][:, j], x1[o][:, j], hr, ALU.add), after=[t2], done="pool_base")
                base = base_store.start(lambda e, j=j: e.dma_start(out_t[b * TPB + j], x1[o][:, j]), after=[t3])
                yield
            last["attnT"] = (tt,)
            x1_free[o] = base_landed[b] = base_store.all_landed()
            v1_free[o] = (("pe_pv", pe.count["pe_pv"]),)
            t = ("dve_stats", dve.count["dve_stats"])
            for j in range(TPB):
                dve.run(lambda e, j=j: e.bn_aggr(mv[:, j], st[:, j]), after=[t, last["mv"]], done="dve_aggr")
            t = ("dve_aggr", dve.count["dve_aggr"])
            last["st"] = t
            steps = [lambda e: e.tensor_tensor(rt[:, 4], mv[:, :, 0], mv[:, :, 0], ALU.mult),
                     lambda e: e.tensor_tensor(rt[:, 4], rt[:, 4], mv[:, :, 1], ALU.add)]
            steps += rsqrt_steps(rstd2, rt[:, 4], rt[:, 1], rt[:, 2], rt[:, 3])
            t = dchain(steps, [t, last["rt"], ("pool_base", pool.count["pool_base"])], "dve_rsqrt")
            last["mv"] = last["rt"] = t
            yield
            for j in range(TPB):
                hr = hrow[:, (b * TPB + j) % NROW, 0:D]
                th = dve.run(lambda e, j=j, hr=hr: e.scalar_tensor_tensor(hr, hr, rstd2[:, j:j + 1], ln2_s, ALU.mult, ALU.mult), after=[t, ln2_t], done="dve_h2")
                i, bk, free = misc.take()

                def tr(e, bk=bk, hr=hr):
                    for k in range(KD):
                        m = e.transpose(bk[:, k * P:(k + 1) * P], hr[:, k * P:(k + 1) * P], ident)
                    return m
                tt = pe.run(tr, after=[th, *free], done="pe_h2T")
                te = act.run(lambda e, bk=bk: e.activation(h2T, bk[:, 0:KD * P].rearrange("p (k t) -> p k t", k=KD), ACT.Copy), after=[tt, last.get("h2T")], done="act_h2T")
                misc.release(i, te)
                i, bk, free = misc.take()

                def mm(e, bk=bk):
                    for k in range(KD):
                        m = e.matmul(bk[:, 0:NE], h2T[:, k], gate_s[:, k], start=(k == 0), stop=(k == KD - 1))
                    return m
                tt = pe.run(mm, after=[te, gate_t, *free], done="pe_gate")
                last["h2T"] = tt
                tl = dve.run(lambda e, bk=bk, j=j: e.tensor_copy(logits[:, b * TPB + j], bk[:, 0:NE]), after=[tt], done="dve_logits")
                misc.release(i, tl)
                yield
            last["logits", b] = tl
            last["h2", b] = th

        block_expert, scattered, base_landed = {}, {}, {}

        def route(gi, mem, mem_free):
            batches = GROUPS[gi]
            t0, nt, nb = batches[0] * TPB, len(batches) * TPB, n_blocks(batches)
            n8 = nt * NE
            top, idx, e1, e2, pos, tot, run_, wts, wk, small, blk = carve(mem, [8, 8, n8, n8, n8, n8, n8, 4 * nt, 2 * nt, 8 * NE, nb + 1])
            lg = logits[:, t0:t0 + nt]
            e1v, e2v, posv, totv, runv = (grid(v, nt) for v in (e1, e2, pos, tot, run_))
            wtv = wts.rearrange("p (a t) -> p a t", a=4)
            l1, l2, q1, q2 = (wtv[:, a] for a in range(4))
            n = "dve_route"
            t = dve.run(lambda e: e.memset(wk, 0.0), after=[last["logits", batches[-1]], *mem_free], done=n)
            for c in range(nt):
                t = dchain([lambda e, c=c: e.max(top, lg[:, c]),
                            lambda e, c=c: e.max_index(idx.bitcast(mybir.dt.uint32), top, lg[:, c]),
                            lambda e, c=c: e.tensor_copy(wtv[:, 0:2, c], top[:, 0:2]),
                            lambda e, c=c: e.tensor_copy(wtv[:, 2:4, c], idx.bitcast(mybir.dt.uint32)[:, 0:2])], [t], n)
                if c % 4 == 3:
                    yield
            iota_e = iota[:, 0:NE].unsqueeze(1).broadcast_to([P, nt, NE])
            d = wk[:, 0:nt]
            t = dchain([lambda e: e.tensor_tensor(e1v, iota_e, q1.unsqueeze(2).broadcast_to([P, nt, NE]), ALU.is_equal),
                        lambda e: e.tensor_tensor(e2v, iota_e, q2.unsqueeze(2).broadcast_to([P, nt, NE]), ALU.is_equal),
                        lambda e: e.tensor_tensor(totv, e1v, e2v, ALU.add),
                        lambda e: e.tensor_copy(run_.bitcast(BF16)[:, 0:n8], tot),
                        lambda e: e.tensor_tensor(d, l2, l1, ALU.subtract)], [t, iota_t], n)
            te = act.run(lambda e: e.activation(d, d, ACT.Exp), after=[t], done="act_route")
            hot = run_.bitcast(BF16)[:, 0:n8]
            i, bk, free = misc.take()

            def mm(e, bk=bk):
                e.matmul(bk[:, 0:n8], before, hot, start=True, stop=True)
                return e.matmul(bk[:, n8:2 * n8], onesb, hot, start=True, stop=True)
            tt = pe.run(mm, after=[t, const_t, *free], done="pe_rank")
            w2c = wk[:, nt:2 * nt]
            cnt, nblk, endb, startb = (small[:, a * NE:(a + 1) * NE] for a in range(4))
            t = dchain([lambda e: e.tensor_scalar(w2c, d, 1.0, None, ALU.add),
                        lambda e: e.reciprocal(l1, w2c),
                        lambda e: e.tensor_tensor(l2, l1, d, ALU.mult),
                        lambda e, bk=bk: e.tensor_copy(pos, bk[:, 0:n8]),
                        lambda e, bk=bk: e.tensor_copy(tot, bk[:, n8:2 * n8])], [te, tt], n)
            misc.release(i, t)
            yield
            ones_nt = onesf[:, 0:nt]
            t = dchain([lambda e, x_=x_: e.tensor_tensor_scan(runv[:, :, x_], ones_nt, totv[:, :, x_], 0.0, ALU.mult, ALU.add) for x_ in range(NE)], [t], n)
            steps = [lambda e: e.tensor_copy(cnt, runv[:, nt - 1]),
                     lambda e: e.tensor_tensor(run_, run_, tot, ALU.subtract),
                     lambda e: e.tensor_tensor(pos, pos, run_, ALU.add)]
            per = nt
            jm = tot[:, 0:per * NE].rearrange("p (e j) -> p e j", e=NE)
            steps += [lambda e: e.tensor_tensor(jm, cnt.unsqueeze(2).broadcast_to([P, NE, per]),
                                                iota128[:, 0:per].unsqueeze(1).broadcast_to([P, NE, per]), ALU.is_gt),
                      lambda e: e.tensor_reduce(nblk, jm, AX.X, ALU.add),
                      lambda e: e.tensor_tensor_scan(endb, onesf[:, 0:NE], nblk, 0.0, ALU.mult, ALU.add),
                      lambda e: e.tensor_tensor(startb, endb, nblk, ALU.subtract),
                      lambda e: e.scalar_tensor_tensor(posv, startb.unsqueeze(1).broadcast_to([P, nt, NE]), float(P), posv, ALU.mult, ALU.add),
                      lambda e: e.tensor_tensor(e1, e1, pos, ALU.mult),
                      lambda e: e.tensor_tensor(e2, e2, pos, ALU.mult),
                      lambda e: e.tensor_reduce(q1, e1v, AX.X, ALU.add),
                      lambda e: e.tensor_reduce(q2, e2v, AX.X, ALU.add),
                      lambda e: e.tensor_copy(d.bitcast(I32), q1),
                      lambda e: e.tensor_copy(w2c.bitcast(I32), q2)]
            t = dchain(steps, [t], n)
            pos_t = t
            yield
            bi = blk[0:1, 0:nb].bitcast(I32)
            acc = blk[0:1, 0:nb]
            steps = [lambda e: e.tensor_scalar(acc, iota[0:1, 0:nb], endb[0:1, 0:1], None, ALU.is_ge)]
            for x_ in range(1, NE - 1):
                steps += [lambda e, x_=x_: e.scalar_tensor_tensor(acc, iota[0:1, 0:nb], endb[0:1, x_:x_ + 1], acc, ALU.is_ge, ALU.add)]
            steps += [lambda e: e.tensor_scalar(bexp[gi], acc, float(2 * FFN), None, ALU.mult)]
            t = dchain(steps, [t], n)
            block_expert[gi] = t
            got = []
            wt_t = None
            for k, (w, at) in enumerate(((l1, d), (l2, w2c))):
                if k:
                    after = [a for a in scatter.all_landed()]
                else:
                    after = []
                wt_t = dve.run(lambda e, w=w: e.tensor_copy(hrow[:, t0 % NROW:t0 % NROW + nt, D + 1], w), after=[pos_t, *after], done="dve_weight")
                for c in range(nt):
                    got.append(scatter.start(lambda e, c=c, at=at: e.indirect_dma_start(
                        rows[gi], bass.IndirectOffsetOnAxis(ap=at.bitcast(I32)[:, c:c + 1], axis=0), hrow[:, (t0 + c) % NROW, :], None),
                        after=[wt_t, pads[gi], last["h2", batches[-1]]]))
                    yield
            scattered[gi] = scatter.all_landed()
            last["routed", gi] = ("dve_route", dve.count["dve_route"])

        def load_w13():
            for k in range(KD):
                for e_ in range(NE):
                    last.setdefault("w13", []).append(weight_load.start(lambda e, k=k, e_=e_: e.dma_start(
                        w13_s[:, k, e_ * 2 * FFN:(e_ + 1) * 2 * FFN], w13T[k * P:(k + 1) * P, e_, :]),
                        after=[last["hT"], ("dve_rope", dve.count["dve_rope"]), ("dve_h", dve.count["dve_h"]), *split_store.all_landed()]))
                    yield

        def load_w2(after):
            for e_ in range(NE):
                last.setdefault("w2", []).append(weight_load.start(lambda e, e_=e_: e.dma_start(
                    w2_mem[:, e_ * KF * D:(e_ + 1) * KF * D].rearrange("p (k n) -> p k n", k=KF), w2T[:, e_, :].rearrange("(k p) n -> p k n", p=P)), after=after))
                yield

        NBLK, NYOUT = 7, 4
        (rb, rhT, rsl, rg, rgT, ry) = carve(stack_mem, [NBLK * RW, 2 * KD * P, 2 * FFN, 2 * FFN, 2 * FFN, NYOUT * D])
        blocks = Ring([rb[:, i * RW:(i + 1) * RW] for i in range(NBLK)])
        blockT = Ring([rhT[:, i * KD * P:(i + 1) * KD * P].rearrange("p (k t) -> p k t", k=KD) for i in range(2)])
        silus = Ring([rsl[:, i * FFN:(i + 1) * FFN] for i in range(2)])
        gated = Ring([rg[:, i * FFN:(i + 1) * FFN] for i in range(2)])
        gatedT = Ring([rgT[:, i * FFN:(i + 1) * FFN] for i in range(2)])
        youts = Ring([ry[:, i * D:(i + 1) * D] for i in range(NYOUT)])
        up_banks = Ring([(bank[0], bank[1]), (bank[2], bank[3])])
        gT_banks = Ring([bank[4]])
        y_bank = Ring([bank[5]])

        def experts(work):
            first = [*last["att_done"]]
            for rg_ in (up_banks, gT_banks, y_bank, blocks, blockT, silus, gated, gatedT, youts):
                rg_.free = [tuple(first)] * len(rg_.buffers)
            n = len(work)
            got, state = {}, {}

            def fetch(w):
                gi, c = work[w]
                i, buf, free = blocks.take()
                got[w] = (i, buf, block_load.start(lambda e, gi=gi, c=c, buf=buf: e.dma_start(buf, rows[gi][c * P:(c + 1) * P, :]),
                                                  after=[*free, *scattered[gi]]))

            def turn(w):
                i, buf, ready = got[w]
                im, bk, free = misc.take()

                def tr(e):
                    for k in range(KD):
                        m = e.transpose(bk[:, k * P:(k + 1) * P], buf[:, k * P:(k + 1) * P], ident)
                    return m
                tt = pe.run(tr, after=[ready, *free], done="pe_blockT")
                ib, bT, bfree = blockT.take()
                te = dve.run(lambda e: e.tensor_copy(bT, bk[:, 0:KD * P].rearrange("p (k t) -> p k t", k=KD)), after=[tt, *bfree], done="dve_blockT")
                misc.release(im, te)
                turned[w] = (ib, bT, te)

            def up(w, half):
                gi, c = work[w]
                if half == 0:
                    iu, banks, free = up_banks.take()
                    ups[w] = (iu, banks)
                iu, banks = ups[w]
                ib, bT, te = turned[w]

                def mm(e):
                    if half == 0:
                        offs[w] = e.value_load(bexp[gi][0:1, c:c + 1], min_val=0, max_val=(NE - 1) * 2 * FFN)
                    for k in range(KD):
                        m = e.matmul(banks[half], bT[:, k], w13_s[:, k, bass.ds(offs[w] + half * FFN, FFN)], start=(k == 0), stop=(k == KD - 1))
                    return m
                tt = pe.run(mm, after=[te, block_expert[gi], *last["w13"], *(free if half == 0 else ())], done="pe_up")
                if half == 0:
                    isl, sl, sfree = silus.take()
                    ts = act.run(lambda e: e.activation(sl, banks[0], ACT.Silu), after=[tt, *sfree], done="act_silu")
                    state[w] = (isl, sl, ts)
                else:
                    isl, sl, ts = state[w]
                    blockT.release(ib, tt)
                    ig, g_, gfree = gated.take()
                    tg = dve.run(lambda e: e.tensor_tensor(g_, banks[1], sl, ALU.mult), after=[ts, tt, *gfree], done="dve_gated")
                    silus.release(isl, tg)
                    up_banks.release(iu, ts, tg)
                    state[w] = (ig, g_, tg)

            def turn_gated(w):
                ig, g_, tg = state[w]
                i, bk, free = gT_banks.take()

                def tr(e):
                    for k in range(KF):
                        m = e.transpose(bk[:, k * P:(k + 1) * P], g_[:, k * P:(k + 1) * P], ident)
                    return m
                tt = pe.run(tr, after=[tg, *free], done="pe_gatedT")
                gated.release(ig, tt)
                it, gT, tfree = gatedT.take()
                te = act.run(lambda e: e.activation(gT, bk, ACT.Copy), after=[tt, *tfree], done="act_gatedT")
                gT_banks.release(i, te)
                state[w] = (it, gT, te)

            def down(w):
                gi, c = work[w]
                it, gT, te = state[w]
                ib, buf, _ = got[w]
                i, bk, free = y_bank.take()

                def mm(e):
                    v = offs[w]
                    for k in range(KF):
                        m = e.matmul(bk[:, 0:D], gT[:, k * P:(k + 1) * P], w2_mem[:, bass.ds(v + k * D, D)], start=(k == 0), stop=(k == KF - 1))
                    return m
                tt = pe.run(mm, after=[te, *last["w2"], *free], done="pe_down")
                gatedT.release(it, tt)
                iy, y, yfree = youts.take()
                ty = dve.run(lambda e: e.tensor_scalar(y, bk[:, 0:D], buf[:, D + 1:D + 2], None, ALU.mult), after=[tt, *yfree], done="dve_y")
                y_bank.release(i, ty)
                ta = add_out.start(lambda e: e.indirect_dma_start(
                    out_rows, bass.IndirectOffsetOnAxis(ap=buf.bitcast(I32)[:, D:D + 1], axis=0), y, None,
                    bounds_check=NBATCH * SEQ - 1, oob_is_err=False, compute_op=ALU.add), after=[ty, *base_landed[GROUPS[gi][-1]]])
                youts.release(iy, ta)
                blocks.release(ib, ta, ty)
            offs, ups, turned = {}, {}, {}
            for w in range(4):
                fetch(w)
            turn(0)
            for w in range(n + 1):
                if w < n:
                    up(w, 0)
                if w >= 1:
                    turn_gated(w - 1)
                if w + 1 < n:
                    turn(w + 1)
                if w < n:
                    up(w, 1)
                if w >= 1:
                    down(w - 1)
                if w + 4 < n:
                    fetch(w + 4)
                yield

        bexp = [sb(f"bexp{i}", [1, n_blocks(g)], I32) for i, g in enumerate(GROUPS)]

        def drain(g):
            for _ in g:
                pass

        def chain(*gs):
            for g in gs:
                yield from g

        def w2_region_free():
            return [last["routed", 0], *scattered[0], *x1_free[0], *v1_free[0], ("pe_square", pe.count["pe_square"]),
                    ("pe_qk", pe.count["pe_qk"]), ("pe_v", pe.count["pe_v"])]

        def pause(n):
            for _ in range(n):
                yield

        def sides(b):
            if b:
                while len(pack_ready[b - 1]) < NKV * QR:
                    yield
                yield from close(b - 1)
            if b + 1 < NBATCH:
                yield from project(b + 1)
            else:
                yield from load_w13()
                yield from route(0, route_a, ())
                yield from pause(10)
                yield from load_w2(w2_region_free())

        groups = [(b, g) for b in range(NBATCH) for g in range(NKV)]
        drain(project(0))
        load_stack(0, 0)
        load_stack(0, 1)
        for r in range(QR):
            drain(max_pass(0, 0, r))
        for n, (b, g) in enumerate(groups):
            if g == 0:
                side, side_n = sides(b), {0: 36, NBATCH - 1: 140}.get(b, 54)
            work = chain(*(attend(b, g, r) for r in range(QR)))
            ahead = chain(*(max_pass(*groups[n + 1], r) for r in range(QR))) if n + 1 < len(groups) else iter(())
            ahead_due = side_due = 0.0
            for k, _ in enumerate(work):
                ahead_due += 42 / 58
                side_due += side_n / 150
                while ahead_due >= 1:
                    next(ahead, None)
                    ahead_due -= 1
                while side_due >= 1:
                    next(side, None)
                    side_due -= 1
                for q in list(norms):
                    if next(q, 0) == 0:
                        norms.remove(q)
                if k == 45 and n + 2 < len(groups):
                    if g == 2 and b + 1 < NBATCH:
                        drain(side)
                    load_stack(*groups[n + 2])
            drain(ahead)
        for q in norms:
            drain(q)
        drain(side)
        last["att_done"] = [(k, pe.count[k]) for k in ("pe_pv", "pe_scores", "pe_max")] + \
                           [(k, act.count[k]) for k in ("act_pv", "act_exp")] + [("dve_max", dve.count["dve_max"])]
        side = chain(close(NBATCH - 1), route(1, probs_mem, last["att_done"]))
        n_first = n_blocks(GROUPS[0])
        every = [(0, c) for c in range(n_first)] + [(1, c) for c in range(n_blocks(GROUPS[1]))]
        for w, _ in enumerate(experts(every)):
            if w < n_first - 6:
                next(side, None)
                next(side, None)
            if w == n_first - 6:
                drain(side)
        pool.wait(*add_out.all_landed())
        sp.wait(*add_out.all_landed(), *base_store.all_landed())

        block = ctx.enter_context(nc.Block())

        @block.sync
        def _(e):
            sp.play(e)

        @block.gpsimd
        def _(e):
            pool.play(e)

        @block.scalar
        def _(e):
            act.play(e)

        @block.vector
        def _(e):
            dve.play(e)

        @block.tensor
        def _(e):
            pe.play(e)


def rope_tables():
    inv_freq = (np.float32(1.0) / np.power(np.float32(THETA), np.arange(0, HD, 2, dtype=np.float32) / np.float32(HD))).astype(np.float32)
    freqs = np.arange(SEQ, dtype=np.float32)[:, None] * inv_freq[None, :]
    cos = np.concatenate([np.cos(freqs)] * 2, axis=1).T
    sin = np.concatenate([-np.sin(freqs), np.sin(freqs)], axis=1).T
    return np.ascontiguousarray(np.tile(cos, (P // HD, 1))), np.ascontiguousarray(np.tile(sin, (P // HD, 1)))


def kernel(L0_attn_x, L0_attn_W_theta, L0_attn_W_phi, L0_attn_W_g, L0_ffn_ln1_w, L0_ffn_ln2_w,
           L0_ffn_wqkv, L0_ffn_wo, L0_ffn_gate_w, L0_ffn_w13, L0_ffn_w2):
    import concourse.bacc as bacc
    from concourse.bass_utils import run_bass_kernel_spmd

    def lay(a):
        return np.ascontiguousarray(np.asarray(a))

    wqkv = np.asarray(L0_ffn_wqkv)
    swap = np.arange(QK).reshape(-1, 2, HD // 2)[:, ::-1].reshape(-1)
    cos, sin = rope_tables()
    tri = np.stack([np.triu(np.ones((P, P), np.float32), 1)] * 2, axis=1)
    ids = np.arange(NTILE * P, dtype=np.int32).reshape(NTILE, P).T
    arrays = {
        "x": lay(L0_attn_x), "wtheta": lay(L0_attn_W_theta), "wphi": lay(L0_attn_W_phi), "wgT": lay(np.asarray(L0_attn_W_g).T),
        "ln1": lay(L0_ffn_ln1_w), "ln2": lay(L0_ffn_ln2_w), "wqkvT": lay(wqkv.T), "wrotT": lay(wqkv[swap].T),
        "woT": lay(np.asarray(L0_ffn_wo).T), "gateT": lay(np.asarray(L0_ffn_gate_w).T),
        "w13T": lay(np.asarray(L0_ffn_w13).transpose(2, 0, 1)), "w2T": lay(np.asarray(L0_ffn_w2).transpose(2, 0, 1)),
        "cos_t": cos, "sin_t": sin, "eye": np.eye(P, dtype=np.float32), "tri": lay(tri), "ids": lay(ids),
    }
    nc = bacc.Bacc("TRN2", target_bir_lowering=False, num_devices=1)
    ins = {f"in_{k}": v for k, v in arrays.items()}
    args = [nc.dram_tensor(k, v.shape, mybir.dt.from_np(v.dtype), kind="ExternalInput").ap() for k, v in ins.items()]
    out = nc.dram_tensor("out_0", [NBATCH, SEQ, D], F32, kind="ExternalOutput").ap()
    mega_kernel(nc, *args, out)
    r = run_bass_kernel_spmd(nc, [ins], core_ids=[0])
    return r.results[0]["out_0"]
```

```python
from contextlib import ExitStack

import numpy as np

import concourse.bass as bass
from concourse import mybir

F32 = mybir.dt.float32
BF16 = mybir.dt.bfloat16
I32 = mybir.dt.int32
ALU = mybir.AluOpType
ACT = mybir.ActivationFunctionType
AX = mybir.AxisListType

P = 128
NBATCH, SEQ, D = 4, 1024, 256
KD = D // P
TPB = SEQ // P
NTILE = NBATCH * TPB
LATENT = 64
NH, NKV, HD = 16, 4, 16
GRP = NH // NKV
QK = (NH + NKV) * HD
QKV = (NH + 2 * NKV) * HD
NE, TOPK, FFN = 8, 2, 512
KF = FFN // P
EPS = 1e-5
CH = 512
QR = SEQ // CH
TPR = CH // P
THETA = 10000.0

KPARTS = (3, 2, 1)
STACK = sum(KPARTS) * HD
NMAX = 2
MASKED = -1e38

GROUPS = ((0, 1, 2), (3,))
RW = D + 2
NOWHERE = 1 << 20


def n_blocks(batches):
    return (TOPK * len(batches) * SEQ + NE * (P - 1)) // P


class Engine:

    def __init__(self, make):
        self.make, self.steps, self.count, self.waited = make, [], {}, {}
        self.latest = None

    def wait(self, *ticks):
        for t in ticks:
            if t is not None and self.waited.get(t[0], 0) < t[1]:
                self.waited[t[0]] = t[1]
                self.steps.append(lambda e, t=t: e.wait_ge(self.make(t[0]), t[1]))

    def run(self, fn, after=(), done=None):
        self.wait(*after)
        if done is None:
            self.steps.append(fn)
            return None
        self.count[done] = self.count.get(done, 0) + 1
        self.steps.append(lambda e: fn(e).then_inc(self.make(done), 1))
        self.latest = (done, self.count[done])
        return self.latest

    def play(self, e):
        for s in self.steps:
            s(e)


class Loads:

    def __init__(self, engine, name, depth):
        self.engine, self.name, self.depth, self.n = engine, name, depth, 0
        self.sent = [0] * depth

    def start(self, *fns, after=()):
        i = self.n % self.depth
        self.n += 1
        sem = f"{self.name}{i}"
        if self.sent[i]:
            self.engine.wait((sem, self.sent[i]))
        self.engine.wait(*after)
        for fn in fns:
            self.engine.steps.append(lambda e, fn=fn: fn(e).then_inc(self.engine.make(sem), 16))
        self.sent[i] += 16 * len(fns)
        return (sem, self.sent[i])

    def all_landed(self):
        return [(f"{self.name}{i}", n) for i, n in enumerate(self.sent) if n]


NORM_PACE = (12, 24)
MAX_PACE = 3
PACK_PACE = 8
SPLIT_PACE = 1
AHEAD = 0.83
SIDE = {0: 1.0, NBATCH - 1: 3.0}
SIDE_ELSE, SIDE_EXPERTS = 1.8, 1.6
STACK_STEP = 45
LATE_STEPS = 10
PAD_BLOCKS, PAD_PACE = 4, 20
WEIGHT_PACE = 8
SCATTER_PACE = (7, 2)
SPARE_BLOCKS = 6


class Ring:

    def __init__(self, buffers):
        self.buffers, self.n = buffers, 0
        self.free = [()] * len(buffers)
        self.taken = set()

    def take(self):
        i = self.n % len(self.buffers)
        self.n += 1
        assert i not in self.taken, "taken again before its last use was noted"
        self.taken.add(i)
        return i, self.buffers[i], self.free[i]

    def release(self, i, *ticks):
        self.free[i] = ticks
        self.taken.discard(i)


def mega_kernel(nc, x, wtheta, wphi, wgT, ln1, ln2, wqkvT, woT, gateT, w13T, w2T,
                rope_q, rope_k, eye, tri, ids, out):
    with ExitStack() as ctx:
        sems = {}

        def make(name):
            if name not in sems:
                sems[name] = ctx.enter_context(nc.semaphore(name))
            return sems[name]

        def sb(name, shape, dt=F32):
            return ctx.enter_context(nc.sbuf_tensor(name, shape, dt))[:]

        pe, act, dve, pool, sp = (Engine(make) for _ in range(5))
        load = Loads(sp, "load", 8)
        split_store = Loads(sp, "split_store", 4)
        stack_load = Loads(sp, "stack_load", 3)
        max_load = Loads(sp, "max_load", 2)
        pack_move = Loads(sp, "pack_move", 3)
        sum_move = Loads(sp, "sum_move", 4)
        base_store = Loads(sp, "base_store", 4)
        weight_load = Loads(sp, "weight_load", 4)
        block_load = Loads(sp, "block_load", 6)
        pad_store = Loads(sp, "pad_store", 2)
        scatter = Loads(pool, "scatter", 6)
        add_out = Loads(pool, "add_out", 1)

        w13_mem = sb("w13_mem", [P, KD * NE * 2 * FFN])
        w2_mem = sb("w2_mem", [P, NE * KF * D])

        def carve(mem, sizes):
            at, views = 0, []
            for n in sizes:
                views.append(mem[:, at:at + n])
                at += n
            assert at <= mem.shape[1], (at, mem.shape)
            return views

        def grid(view, a):
            return view.rearrange("p (a b) -> p a b", a=a)

        (xn_f, xnT_f, h_f, hT_f, gram_f, gw_f, mix_f, cosT, sinT, rot1, rot2, qk32, qres, split_f, cosK) = carve(
            w13_mem, [TPB * D, KD * SEQ, TPB * D, KD * SEQ, KD * D, KD * D, KD * D, SEQ, SEQ, CH, CH, CH, CH, 2 * 3 * CH // 2, SEQ])
        xn, xnT, h, hT = grid(xn_f, TPB), grid(xnT_f, KD), grid(h_f, TPB), grid(hT_f, KD)
        gram, gw, mix = grid(gram_f, KD), grid(gw_f, KD), grid(mix_f, KD)
        splits = Ring([s.rearrange("p (s q) -> p s q", s=3) for s in (
            split_f.bitcast(BF16)[:, 0:3 * CH], split_f.bitcast(BF16)[:, 3 * CH:6 * CH])])
        (wgT_f, pair_f, wqkv_f, x_even, v_even, rot3, rot4, route_a) = carve(
            w2_mem, [KD * D, KD * D, KD * QKV, TPB * D, TPB * NKV * 32, CH, CH, 1700])
        rots, sinK = [(rot1, rot2), (rot3, rot4)], route_a[:, RW:RW + SEQ]
        wgT_s, pairT, wqkv_s = grid(wgT_f, KD), grid(pair_f, KD), grid(wqkv_f, KD)
        x1 = [grid(x_even, TPB), grid(sb("x_odd", [P, TPB * D]), TPB)]
        v1_flat = [v_even, sb("v_odd", [P, TPB * NKV * 32])]
        v1 = [v.rearrange("p (t g c) -> p t g c", t=TPB, g=NKV) for v in v1_flat]

        w13_s = w13_mem.rearrange("p (k n) -> p k n", k=KD)
        NSTACK, stack_n = 3, (GRP + 1) * SEQ
        stack_mem = sb("stack_mem", [P, NSTACK * stack_n // 2])
        stack = [stack_mem.bitcast(BF16)[:, i * stack_n:(i + 1) * stack_n].rearrange("p (h t) -> p h t", h=GRP + 1)
                 for i in range(NSTACK)]
        probs_mem = sb("probs_mem", [P, 2 * GRP * CH])
        probs = Ring([p.rearrange("p (h q) -> p h q", h=GRP) for p in (probs_mem[:, 0:GRP * CH], probs_mem[:, GRP * CH:])])
        NROW = max(len(g) for g in GROUPS) * TPB
        hrow = sb("hrow", [P, NROW * RW]).rearrange("p (t c) -> p t c", t=NROW)
        attnT = sb("attnT", [P, KD * SEQ]).rearrange("p (k t) -> p k t", k=KD)
        heads_out = Ring([sb("heads_out0", [P, CH]), sb("heads_out1", [P, CH])])
        recip_rows = sb("recip_rows", [P, CH])
        sums = Ring([sb("sums0", [P, GRP * CH // P]), sb("sums1", [P, GRP * CH // P])])
        yrow = sb("yrow", [P, D])
        wo_s = sb("wo_s", [P, KD * D]).rearrange("p (k n) -> p k n", k=KD)
        gate_s = sb("gate_s", [P, KD * NE]).rearrange("p (k n) -> p k n", k=KD)
        ln1_s = sb("ln1_s", [P, KD])
        ln2_s = sb("ln2_s", [P, D])
        ident = sb("ident", [P, P])
        identb = sb("identb", [P, P], BF16)
        causal = sb("causal", [P, P], BF16)
        before = sb("before", [P, P], BF16)
        onesb = sb("onesb", [P, P], BF16)
        st = sb("st", [P, TPB * 6]).rearrange("p (t c) -> p t c", t=TPB)
        mv = sb("mv", [P, TPB * 2]).rearrange("p (t c) -> p t c", t=TPB)
        rt = sb("rt", [P, 6 * TPB]).rearrange("p (a t) -> p a t", a=6)
        rstd, mean1, scale1 = (sb(n, [P, 2 * TPB]).rearrange("p (b t) -> p b t", b=2) for n in ("rstd", "mean1", "scale1"))
        rstd2 = sb("rstd2", [P, TPB])
        mx = sb("mx", [P, 2 * 16]).rearrange("p (c n) -> p c n", c=2)
        mxc = sb("mxc", [P, 16])
        mneg = sb("mneg", [16, P])
        mneg_parts = sb("mneg_parts", [16, NMAX * P], BF16).rearrange("p (s q) -> p s q", s=NMAX)
        h2T = sb("h2T", [P, KD * P]).rearrange("p (k t) -> p k t", k=KD)
        logits = sb("logits", [P, NTILE * NE]).rearrange("p (t e) -> p t e", t=NTILE)
        ids_s = sb("ids_s", [P, NTILE], I32)

        bank = [ctx.enter_context(nc.psum_tensor(f"bank{i}", [P, CH], F32))[:] for i in range(8)]
        pv_bank = Ring([bank[5]])
        misc = max_banks = score_banks = Ring([b for b in bank if b is not bank[5]])

        recips = nc.dram_tensor("recips", [NBATCH * NKV * QR, GRP, CH], F32, kind="Internal").ap()
        parts = [nc.dram_tensor(f"qk_parts{b}", [3, QK, SEQ], BF16, kind="Internal").ap() for b in range(NBATCH)]
        rows = [nc.dram_tensor(f"routed{i}", [n_blocks(g) * P, RW], F32, kind="Internal").ap() for i, g in enumerate(GROUPS)]
        x_v = x.rearrange("b (j p) d -> b p j d", p=P)
        out_t = out.rearrange("b (j p) d -> (b j) p d", p=P)
        out_rows = out.rearrange("b n d -> (b n) d")

        def kview(w):
            return w.rearrange("(k p) n -> p k n", p=P)

        HALVES = [slice(0, TPB // 2), slice(TPB // 2, TPB)]
        x_tick = {}

        x1_free = [(), ()]
        v1_free = [(), ()]

        def load_x(b):
            halves = [load.start(lambda e, s=s: e.dma_start(x1[b % 2][:, s], x_v[b][:, s]), after=x1_free[b % 2]) for s in HALVES]
            x_tick[b] = [halves[j // (TPB // 2)] for j in range(TPB)]

        load_x(0)
        eye_t = load.start(lambda e: e.dma_start(ident, eye))
        wt_f, wp_f = h_f[0:LATENT, 0:D], h_f[0:LATENT, D:2 * D]
        tp_t = [load.start(lambda e: e.dma_start(wt_f, wtheta)), load.start(lambda e: e.dma_start(wp_f, wphi))]
        wg_t = load.start(lambda e: e.dma_start(wgT_s, kview(wgT)))
        wqkv_t = [load.start(lambda e: e.dma_start(wqkv_s, kview(wqkvT))),
                  load.start(lambda e: e.dma_start(ln1_s, ln1.rearrange("(k p) -> p k", p=P), allow_slow_non_contiguous=True))]
        rope_t = [load.start(lambda e, dst=dst, src=src: e.dma_start(dst, src)) for dst, src in (
            (cosT, rope_q[0]), (sinT, rope_q[1]), (cosK[0:NKV * HD, :], rope_k[0]), (sinK[0:NKV * HD, :], rope_k[1]))]
        tri_in = recip_rows[:, 0:2 * P]
        tri_t = load.start(lambda e: e.dma_start(tri_in.rearrange("p (a b) -> p a b", a=2), tri))
        ids_t = load.start(lambda e: e.dma_start(ids_s, ids))
        ln2_t = load.start(lambda e: e.dma_start(ln2_s, ln2.partition_broadcast(P)))
        wo_t = load.start(lambda e: e.dma_start(wo_s, kview(woT)))
        gate_t = load.start(lambda e: e.dma_start(gate_s, kview(gateT)))

        def pool_set(fn, after=()):
            n = pool.count.get("pool_set", 0)
            return pool.run(fn, after=[*after, ("pool_set", n)], done="pool_set")

        pad = route_a[:, 0:RW]
        pool_set(lambda e: e.memset(pad, 0.0))
        pad_set = pool_set(lambda e: e.memset(pad.bitcast(I32)[:, D:D + 1], NOWHERE))
        for v in v1_flat:
            pool_set(lambda e, v=v: e.memset(v, 0.0))
        for v in v1:
            v_set = pool_set(lambda e, v=v: e.memset(v[:, :, :, HD:HD + 1], 1.0))
        for s in stack:
            ones_set = pool_set(lambda e, s=s: e.memset(s[STACK:STACK + NMAX, GRP, :], 1.0))
        pads = [[] for _ in rows]

        def fill_rows():
            for gi, r in enumerate(rows):
                blocks_v = r.rearrange("(n p) c -> p n c", p=P)
                for n0 in range(0, blocks_v.shape[1], PAD_BLOCKS):
                    to = blocks_v[:, n0:min(n0 + PAD_BLOCKS, blocks_v.shape[1])]
                    pads[gi].append(pad_store.start(lambda e, to=to: e.dma_start(
                        to, pad.unsqueeze(1).broadcast_to([P, to.shape[1], RW])), after=[pad_set]))
                    yield

        hrow_i = hrow.bitcast(I32)
        ids_set = pool_set(lambda e: e.tensor_copy(hrow_i[:, :, D], ids_s[:, 0:NROW]), after=[ids_t])
        iota = sb("iota", [P, 96])
        iota128 = sb("iota128", [P, NTILE])
        onesf = sb("onesf", [P, NTILE])
        pool_set(lambda e: e.iota(iota, pattern=[[1, 96]], base=0, channel_multiplier=0, allow_small_or_imprecise_dtypes=True))
        pool_set(lambda e: e.iota(iota128, pattern=[[P, NTILE]], base=0, channel_multiplier=0, allow_small_or_imprecise_dtypes=True))
        iota_t = pool_set(lambda e: e.memset(onesf, 1.0))

        i, bk, free = misc.take()

        def pair_mm(e, bk=bk):
            for k in range(KD):
                m = e.matmul(bk[:, k * D:(k + 1) * D], wp_f[:, k * P:(k + 1) * P], wt_f, start=True, stop=True)
            return m
        t = pe.run(pair_mm, after=tp_t, done="pe_pair")
        pair_ready = act.run(lambda e, bk=bk: e.activation(pairT, grid(bk, KD), ACT.Copy, scale=float(D) ** -0.5), after=[t], done="act_pair")
        misc.release(i, pair_ready)

        def dve_prepare():
            dve.run(lambda e: e.tensor_copy(identb, ident), after=[eye_t], done="dve_const")
            dve.run(lambda e: e.tensor_scalar(causal, tri_in[:, 0:P], MASKED, None, ALU.mult), after=[tri_t], done="dve_const")
            dve.run(lambda e: e.tensor_copy(before, tri_in[:, P:2 * P]), done="dve_const")
            const_t = dve.run(lambda e: e.memset(onesb, 1.0), done="dve_const")
            for k in range(KD):
                wq_ready = dve.run(lambda e, k=k: e.tensor_scalar(wqkv_s[:, k], wqkv_s[:, k], ln1_s[:, k:k + 1], None, ALU.mult), after=wqkv_t, done="dve_wqkv")
            return const_t, wq_ready

        def slowly(fns, after, name):
            t = None
            for f in fns:
                t = dve.run(f, after=[*after, t] if t else after, done=name)
                yield
            return t

        def pause(n):
            for _ in range(n):
                yield

        def rsqrt_steps(dst, var, a, u, w):
            ai, ui, di = a.bitcast(I32), u.bitcast(I32), dst.bitcast(I32)
            steps = [lambda e: e.tensor_scalar(a, var, EPS, None, ALU.add),
                     lambda e: e.tensor_scalar(ui, ai, 1, None, ALU.logical_shift_right),
                     lambda e: e.tensor_scalar(di, ui, -1.0, float(0x5F3759DF), ALU.mult, ALU.add)]
            for _ in range(3):
                steps += [lambda e: e.scalar_tensor_tensor(u, dst, -0.5, a, ALU.mult, ALU.mult),
                          lambda e: e.tensor_tensor(w, u, dst, ALU.mult),
                          lambda e: e.scalar_tensor_tensor(dst, w, 1.5, dst, ALU.add, ALU.mult)]
            return steps

        x1_ready, v_ready, parts_ready = {}, {}, {}
        last = {}

        def project(b):
            o = b % 2
            xb = x1[o]
            if b not in x_tick:
                load_x(b)
            for j in range(TPB):
                dve.run(lambda e, j=j: e.bn_stats(st[:, j], xb[:, j]), after=[x_tick[b][j], last.get("st")], done="dve_stats")
                yield
            t = ("dve_stats", dve.count["dve_stats"])
            for j in range(TPB):
                dve.run(lambda e, j=j: e.bn_aggr(mv[:, j], st[:, j]), after=[t, last.get("mv")], done="dve_aggr")
                yield
            t = last["st"] = ("dve_aggr", dve.count["dve_aggr"])
            t = yield from slowly(rsqrt_steps(rt[:, 0], mv[:, :, 1], rt[:, 1], rt[:, 2], rt[:, 3]), [t, last.get("rt")], "dve_rsqrt")
            yield
            xn_at = []
            for j in range(TPB):
                xn_t = dve.run(lambda e, j=j: e.tensor_scalar(xn[:, j], xb[:, j], mv[:, j, 0:1], rt[:, 0, j:j + 1], ALU.subtract, ALU.mult),
                               after=[t, last.get("xn")], done="dve_xn")
                xn_at.append(xn_t)
                yield "xn" if j == TPB - 1 else None
            last["mv"] = last["rt"] = xn_t
            for c0 in range(0, TPB * KD, 4):
                i, bk, free = misc.take()

                def tr(e, c0=c0, bk=bk):
                    for c in range(4):
                        j, k = c0 // KD + c % 2, c // 2
                        m = e.transpose(bk[:, c * P:(c + 1) * P], xn[:, j, k * P:(k + 1) * P], ident)
                    return m
                tt = pe.run(tr, after=[xn_at[c0 // KD + 1], *free, eye_t, last.get("xnT")], done="pe_xnT")
                xnT_t = act.run(lambda e, c0=c0, bk=bk: e.activation(
                    xnT[:, :, c0 // KD * P:(c0 // KD + 2) * P], bk.rearrange("p (k t) -> p k t", k=KD), ACT.Copy), after=[tt], done="act_xnT")
                misc.release(i, xnT_t)
                yield
            i, bk, free = misc.take()
            for k in range(KD):
                def gm(e, k=k, bk=bk):
                    for j in range(TPB):
                        m = e.matmul(bk[:, k * D:(k + 1) * D], xn[:, j, k * P:(k + 1) * P], xn[:, j], start=(j == 0), stop=(j == TPB - 1))
                    return m
                t = pe.run(gm, after=[xn_t, *free], done="pe_gram")
                yield
            gram_t = act.run(lambda e, bk=bk: e.activation(gram, grid(bk, KD), ACT.Copy), after=[t], done="act_gram")
            misc.release(i, gram_t)
            last["xn"] = t

            def square(lhs, rhs, dst, after):
                i, bk, free = misc.take()

                def mm(e, bk=bk):
                    for r in range(KD):
                        for k in range(KD):
                            m = e.matmul(bk[:, r * D:(r + 1) * D], lhs[:, k, r * P:(r + 1) * P], rhs[:, k], start=(k == 0), stop=(k == KD - 1))
                    return m
                t = pe.run(mm, after=[*after, *free], done="pe_square")
                t = act.run(lambda e, bk=bk: e.activation(dst, grid(bk, KD), ACT.Copy), after=[t], done="act_square")
                misc.release(i, t)
                return t
            t = square(gram, wgT_s, gw, [gram_t, wg_t])
            yield from pause(3)
            mix_t = square(pairT, gw, mix, [t, pair_ready])
            yield from pause(3)
            for j0 in range(0, TPB, 2):
                i, bk, free = misc.take()

                def mm(e, j0=j0, bk=bk):
                    for c in range(2):
                        for k in range(KD):
                            m = e.matmul(bk[:, c * D:(c + 1) * D], xnT[:, k, (j0 + c) * P:(j0 + c + 1) * P], mix[:, k], start=(k == 0), stop=(k == KD - 1))
                    return m
                tt = pe.run(mm, after=[mix_t, xnT_t, *free], done="pe_x1")
                x1_t = dve.run(lambda e, j0=j0, bk=bk: e.tensor_tensor(xb[:, j0:j0 + 2], grid(bk, 2), xb[:, j0:j0 + 2], ALU.add), after=[tt], done="dve_x1")
                misc.release(i, x1_t)
                yield
                for j in (j0, j0 + 1):
                    dve.run(lambda e, j=j: e.bn_stats(st[:, j], xb[:, j]), after=[x1_t, last["st"]], done="dve_stats")
                    yield
            last["xnT"] = tt
            t = ("dve_stats", dve.count["dve_stats"])
            for j in range(TPB):
                dve.run(lambda e, j=j: e.bn_aggr(mv[:, j], st[:, j]), after=[t, last["mv"]], done="dve_aggr")
                yield
            t = ("dve_aggr", dve.count["dve_aggr"])
            last["st"] = t
            steps = rsqrt_steps(rstd[:, o], mv[:, :, 1], rt[:, 1], rt[:, 2], rt[:, 3])
            steps += [lambda e: e.tensor_copy(mean1[:, o], mv[:, :, 0]),
                      lambda e: e.tensor_tensor(rt[:, 4], rstd[:, o], rstd[:, o], ALU.mult),
                      lambda e: e.tensor_tensor(rt[:, 4], rt[:, 4], mv[:, :, 1], ALU.mult)]
            steps += rsqrt_steps(rt[:, 0], rt[:, 4], rt[:, 1], rt[:, 2], rt[:, 3])
            steps += [lambda e: e.tensor_tensor(scale1[:, o], rt[:, 0], rstd[:, o], ALU.mult)]
            t = yield from slowly(steps, [t, last["rt"], *x1_free[o]], "dve_rsqrt")
            x1_ready[b] = last["rt"] = last["mv"] = t
            yield
            h_at = []
            for j in range(TPB):
                h_t = dve.run(lambda e, j=j: e.tensor_scalar(h[:, j], xb[:, j], mean1[:, o, j:j + 1], scale1[:, o, j:j + 1], ALU.subtract, ALU.mult),
                              after=[t, last.get("h"), ("pe_pair", 1)], done="dve_h")
                h_at.append(h_t)
                yield
            for c0 in range(0, TPB * KD, 4):
                i, bk, free = misc.take()

                def tr(e, c0=c0, bk=bk):
                    for c in range(4):
                        j, k = c0 // KD + c % 2, c // 2
                        m = e.transpose(bk[:, c * P:(c + 1) * P], h[:, j, k * P:(k + 1) * P], ident)
                    return m
                tt = pe.run(tr, after=[h_at[c0 // KD + 1], *free], done="pe_hT")
                hT_t = act.run(lambda e, c0=c0, bk=bk: e.activation(
                    hT[:, :, c0 // KD * P:(c0 // KD + 2) * P], bk.rearrange("p (k t) -> p k t", k=KD), ACT.Copy), after=[tt, last.get("hT")], done="act_hT")
                misc.release(i, hT_t)
                yield
            last["h"] = tt
            i, bk, free = misc.take()

            def vm(e, bk=bk):
                for j in range(TPB):
                    for k in range(KD):
                        m = e.matmul(bk[:, j * NKV * HD:(j + 1) * NKV * HD], hT[:, k, j * P:(j + 1) * P], wqkv_s[:, k, QK:QKV], start=(k == 0), stop=(k == KD - 1))
                return m
            tt = pe.run(vm, after=[hT_t, wq_ready, *free], done="pe_v")
            v_ready[b] = act.run(lambda e, bk=bk: e.activation(
                v1[o][:, :, :, 0:HD], bk.rearrange("p (t g c) -> p t g c", t=TPB, g=NKV), ACT.Copy),
                after=[tt, v_set, *v1_free[o]], done="act_v")
            misc.release(i, v_ready[b])
            yield
            def product(r0, n, cols):
                i, bk, free = misc.take()

                def mm(e):
                    for k in range(KD):
                        m = e.matmul(bk[0:n, :], wqkv_s[:, k, r0:r0 + n], hT[:, k, cols], start=(k == 0), stop=(k == KD - 1))
                    return m
                return i, bk, pe.run(mm, after=[hT_t, wq_ready, *free], done="pe_qk")

            def rotated(which, parts_, after):
                for dst, to, bank_rows, table in parts_:
                    t = dve.run(lambda e, dst=dst, to=to, bank_rows=bank_rows, table=table: e.tensor_tensor(
                        rots[which][dst][to], bank_rows, table, ALU.mult), after=[*after, last.get(("rot", which)), *rope_t], done="dve_rope")
                return t

            def split(which, op, n, r0, cols, after):
                r1, r2 = rots[which]
                i, sp3, free = splits.take()
                adder, name = (dve, "dve_split") if b == 0 else (pool, "pool_split")
                t = adder.run(lambda e: e.tensor_tensor(qk32[0:n], r1[0:n], r2[0:n], op), after=[after, last.get("qk32")], done=name)
                last["rot", which] = t
                yield from pause(SPLIT_PACE)
                th = act.run(lambda e: e.activation(sp3[0:n, 0], qk32[0:n], ACT.Copy), after=[t, *free], done="act_split")
                yield from pause(SPLIT_PACE)
                tr_ = pool.run(lambda e: e.tensor_tensor(qres[0:n], qk32[0:n], sp3[0:n, 0], ALU.subtract), after=[th, last.get("qres")], done="pool_split")
                last["qk32"] = tr_
                yield from pause(SPLIT_PACE)
                tm = act.run(lambda e: e.activation(sp3[0:n, 1], qres[0:n], ACT.Copy), after=[tr_], done="act_split")
                yield from pause(SPLIT_PACE)
                tl = adder.run(lambda e: e.tensor_tensor(sp3[0:n, 2], qres[0:n], sp3[0:n, 1], ALU.subtract), after=[tm], done=name)
                last["qres"] = tl
                ts = split_store.start(lambda e: e.dma_start(parts[b][:, r0:r0 + n, cols].rearrange("s r t -> r s t"), sp3[0:n]), after=[tl, tm])
                splits.release(i, ts)
                parts_ready.setdefault(b, []).append(ts)

            HK = NKV * HD // 2
            def k_rows(cols):
                i, bk, tt = product(NH * HD, 2 * HK, cols)
                lo, hi = slice(0, HK), slice(HK, 2 * HK)
                t = rotated(0, ((0, slice(0, 2 * HK), bk[0:2 * HK, :], cosK[0:2 * HK, cols]),
                                (1, lo, bk[hi, :], sinK[lo, cols]), (1, hi, bk[lo, :], sinK[hi, cols])), [tt])
                misc.release(i, t)
                yield
                yield from split(0, ALU.add, 2 * HK, NH * HD, cols, t)

            def q_products(cols):
                i1, first, t1 = product(0, P, cols)
                yield
                i2, second, t2 = product(P, P, cols)
                every = slice(0, P)
                q_done.append(rotated(1, ((0, every, first, cosT[:, cols]), (1, every, second, sinT[:, cols])), [t1, t2]))
                q_done.append(rotated(0, ((0, every, second, cosT[:, cols]), (1, every, first, sinT[:, cols])), [t1, t2]))
                misc.release(i1, q_done[-1])
                misc.release(i2, q_done[-1])
                last["hT"] = t2
                yield

            for c in range(QR):
                cols, q_done = slice(c * CH, (c + 1) * CH), []
                yield from k_rows(cols)
                yield from q_products(cols)
                yield from split(1, ALU.subtract, P, 0, cols, q_done[0])
                yield from split(0, ALU.add, P, P, cols, q_done[1])
                yield ("rows", c)

        stack_ready, stack_free = {}, [()] * NSTACK
        max_ready = {}

        def load_stack(b, g):
            s = stack[(b * NKV + g) % NSTACK]
            free = stack_free[(b * NKV + g) % NSTACK]
            lot, at = [], 0
            for qp, nk in enumerate(KPARTS):
                to = slice(at * HD, (at + nk) * HD)
                at += nk
                lot.append(lambda e, to=to, qp=qp, nk=nk: e.dma_start(
                    s[to, 0:GRP, :].rearrange("p h t -> p (h t)"),
                    q_rows(b, qp)[g].rearrange("i h t -> i (h t)").unsqueeze(0).broadcast_to([nk, HD, GRP * SEQ])))
                lot.append(lambda e, to=to, nk=nk: e.dma_start(
                    s[to, GRP, :], parts[b][0:nk, NH * HD + g:QK:NKV, :]))
            ready = stack_load.start(*lot, after=[*parts_ready[b], *free])
            stack_ready[b, g] = [[ready]] * QR

        def q_rows(b, qp):
            return parts[b][qp, 0:NH * HD, :].rearrange("(i g h) t -> g i h t", g=NKV, h=GRP)

        def load_first_stack(r):
            cols, lot, at = slice(r * CH, (r + 1) * CH), [], 0
            for qp, nk in enumerate(KPARTS):
                lot.append(lambda e, to=slice(at * HD, (at + nk) * HD), nk=nk: e.dma_start(
                    stack[0][to, GRP, cols], parts[0][0:nk, NH * HD:QK:NKV, cols]))
                for _ in range(nk):
                    lot.append(lambda e, to=slice(at * HD, (at + 1) * HD), qp=qp: e.dma_start(
                        stack[0][to, 0:GRP, cols], q_rows(0, qp)[0][:, :, cols]))
                    at += 1
            ready = stack_load.start(*lot, after=parts_ready[0])
            stack_ready.setdefault((0, 0), []).append([*(stack_ready[0, 0][-1] if r else ()), ready])

        def max_pass(b, g, r):
            s = stack[(b * NKV + g) % NSTACK]
            units = []
            for jj in range(TPR):
                j = r * TPR + jj
                if r:
                    units += [(j, 0, CH, [hh], False, 0) for hh in range(GRP)]
                w = (jj + 1) * P
                nh = {1: 4, 2: 2}.get(jj + 1, 1)
                units += [(j, r * CH, w, list(range(h0, h0 + nh)), True, 1 if r else 0) for h0 in range(0, GRP, nh)]
            for j, k0, w, heads, diag, chunk in units:
                i, bk, free = max_banks.take()

                def mm(e, j=j, k0=k0, w=w, heads=heads, diag=diag, bk=bk):
                    for c, hh in enumerate(heads):
                        m = e.matmul(bk[:, c * w:(c + 1) * w], s[0:STACK, hh, j * P:(j + 1) * P], s[0:STACK, GRP, k0:k0 + w], start=True, stop=not diag)
                        if diag:
                            m = e.matmul(bk[:, (c + 1) * w - P:(c + 1) * w], identb, causal, start=False, stop=True)
                    return m
                t = pe.run(mm, after=[*stack_ready[b, g][r], const_t, *free], done="pe_max")
                to = mx[:, chunk, :].rearrange("p (h j) -> p h j", h=GRP)[:, heads[0]:heads[-1] + 1, j % TPR]
                t = dve.run(lambda e, w=w, n=len(heads), bk=bk, to=to: e.tensor_reduce(
                    to, bk[:, 0:n * w].rearrange("p (h k) -> p h k", h=n), AX.X, ALU.max), after=[t, last.get("mx")], done="dve_max")
                max_banks.release(i, t)
                yield
            yield from pause(MAX_PACE)
            if r:
                src = mxc
                t = dve.run(lambda e: e.tensor_tensor(mxc, mx[:, 0], mx[:, 1], ALU.max), after=[t, last.get("mxc")], done="dve_max")
                last["mx"] = t
            else:
                src = mx[:, 0]
            i, bk, free = misc.take()
            tt = pe.run(lambda e, bk=bk: e.transpose(bk[0:16, 0:P], src, ident), after=[t, *free], done="pe_maxT")
            last["mxc" if r else "mx"] = tt
            t1 = dve.run(lambda e, bk=bk: e.tensor_scalar(mneg, bk[0:16, 0:P], -1.0, None, ALU.mult), after=[tt], done="dve_neg")
            misc.release(i, t1)
            t2 = dve.run(lambda e: e.tensor_copy(mneg_parts[:, 0], mneg), after=[t1, *last.get("mneg", ())], done="dve_neg")
            t3 = dve.run(lambda e: e.tensor_tensor(mneg_parts[:, 1], mneg, mneg_parts[:, 0], ALU.subtract), after=[t2], done="dve_neg")
            got = [max_load.start(*[lambda e, c=c, hh=hh: e.dma_start(
                s[STACK + c:STACK + c + 1, hh, r * CH:(r + 1) * CH],
                mneg_parts[hh * TPR:(hh + 1) * TPR, c, :]) for c in range(NMAX) for hh in range(GRP)], after=[t3])]
            last["mneg"] = got
            max_ready[b, g, r] = got
            yield

        pack_ready = {}
        held = []
        norms, normalised = [], []
        def attend(b, g, r):
            o = b % 2
            s = stack[(b * NKV + g) % NSTACK]
            bank_of = {}
            nk = (r + 1) * TPR

            def pv_mm(kt, ip, pb, q0, ready):
                if kt == 0:
                    bank_of["pv"] = pv_bank.take()
                ipv, pv, pv_free = bank_of["pv"]

                def mm(e):
                    for hh in range(GRP):
                        m = e.matmul(pv[32 * hh:32 * hh + 32, q0:CH], v1[o][:, kt, g, :], pb[:, hh, q0:CH], start=(kt == 0), stop=(kt == nk - 1))
                    return m
                t = pe.run(mm, after=[*ready, v_ready[b], *(pv_free if kt == 0 else ())], done="pe_pv")
                probs.release(ip, t)
                if kt == nk - 1:
                    i, ho, free = heads_out.take()
                    t = act.run(lambda e: e.activation(ho, pv, ACT.Copy), after=[t, *free], done="act_pv")
                    pv_bank.release(ipv, t)
                    norms.append(normalise(b, g, r, i, ho, t))
            for kt in range(nk):
                q0 = max(kt * P - r * CH, 0)
                ip, pb, p_free = probs.take()
                for hh in range(GRP):
                    i, bk, free = score_banks.take()
                    t = pe.run(lambda e, kt=kt, hh=hh, q0=q0, bk=bk: e.matmul(
                        bk[:, q0:CH], s[0:STACK + NMAX, GRP, kt * P:(kt + 1) * P], s[0:STACK + NMAX, hh, r * CH + q0:(r + 1) * CH], start=True, stop=True),
                        after=[*max_ready[b, g, r], ones_set, *free], done="pe_scores")
                    score_t = t
                    t = act.run(lambda e, hh=hh, q0=q0, bk=bk, pb=pb: e.activation(pb[:, hh, q0:CH], bk[:, q0:CH], ACT.Exp, scale=float(HD) ** -0.5),
                                after=[t, *(p_free if hh == 0 else ())], done="act_exp")
                    score_banks.release(i, t)
                    yield
                ready = [t]
                if kt >= r * TPR:
                    t = pool.run(lambda e, q0=q0, pb=pb: e.affine_select(
                        pb[:, :, q0:q0 + P], pb[:, :, q0:q0 + P], [[0, GRP], [1, P]], ALU.is_ge, 0.0, base=0, channel_multiplier=-1),
                        after=[t], done="pool_causal")
                    ready.append(t)
                held.append(lambda kt=kt, ip=ip, pb=pb, q0=q0, ready=ready: pv_mm(kt, ip, pb, q0, ready))
                if len(held) > 1:
                    held.pop(0)()
                    yield
            if r == QR - 1:
                stack_free[(b * NKV + g) % NSTACK] = (score_t, ("pe_max", pe.count["pe_max"]))
            yield

        def normalise(b, g, r, i, ho, ho_t):
            n = (b * NKV + g) * QR + r
            isum, sm, free = sums.take()
            t = sum_move.start(lambda e: e.dma_start(sm, ho[HD:P:32, :]), after=[ho_t, *free])
            yield from pause(NORM_PACE[0])
            t = dve.run(lambda e: e.reciprocal(sm, sm), after=[t], done="dve_recip")
            t = sum_move.start(lambda e: e.dma_start(recips[n].rearrange("h (p c) -> (h p) c", c=sm.shape[1]), sm), after=[t])
            sums.release(isum, t)
            while len(normalised) < n:
                yield
            t = sum_move.start(lambda e: e.dma_start(recip_rows, recips[n].unsqueeze(1).broadcast_to([GRP, 32, CH])), after=[t, const_t, last.get("recip_rows")])
            yield from pause(NORM_PACE[1])
            t = last["recip_rows"] = dve.run(lambda e: e.tensor_tensor(ho, ho, recip_rows, ALU.mult), after=[t], done="dve_norm")
            k, row = divmod(g * GRP * HD, P)
            t = pack_move.start(*[lambda e, hh=hh: e.dma_start(
                attnT[row + hh * HD:row + (hh + 1) * HD, k, r * CH:(r + 1) * CH], ho[32 * hh:32 * hh + HD, :]) for hh in range(GRP)],
                after=[t, *last.get("attnT", ())])
            heads_out.release(i, t)
            pack_ready.setdefault(b, []).append(t)
            normalised.append(n)
            yield

        def close(b):
            o = b % 2
            first, rows_free = ids_set, []
            if b == GROUPS[1][0]:
                rows_free = scattered[0]
                first = pool_set(lambda e: e.tensor_copy(hrow_i[:, 0:NTILE - NROW, D], ids_s[:, NROW:NTILE]), after=rows_free)
            for j in range(TPB):
                i, bk, free = misc.take()

                def mm(e, j=j, bk=bk):
                    for k in range(KD):
                        m = e.matmul(bk[:, 0:D], attnT[:, k, j * P:(j + 1) * P], wo_s[:, k], start=(k == 0), stop=(k == KD - 1))
                    return m
                tt = pe.run(mm, after=[*pack_ready[b], wo_t, *free], done="pe_wo")
                hr = hrow[:, (b * TPB + j) % NROW, 0:D]
                t1 = dve.run(lambda e, j=j: e.tensor_scalar(yrow, x1[o][:, j], mean1[:, o, j:j + 1], rstd[:, o, j:j + 1], ALU.subtract, ALU.mult), after=[x1_ready[b], last.get("yrow")], done="dve_x2")
                t2 = dve.run(lambda e, bk=bk, hr=hr: e.tensor_tensor(hr, bk[:, 0:D], yrow, ALU.add), after=[tt, t1, first, *rows_free], done="dve_x2")
                last["yrow"] = t2
                misc.release(i, t2)
                dve.run(lambda e, j=j, hr=hr: e.bn_stats(st[:, j], hr), after=[t2, last.get("st")], done="dve_stats")
                yield
                t3 = pool.run(lambda e, j=j, hr=hr: e.tensor_tensor(x1[o][:, j], x1[o][:, j], hr, ALU.add), after=[t2], done="pool_base")
                base = base_store.start(lambda e, j=j: e.dma_start(out_t[b * TPB + j], x1[o][:, j]), after=[t3])
                yield
            last["attnT"] = (tt,)
            x1_free[o] = base_landed[b] = base_store.all_landed()
            v1_free[o] = (("pe_pv", pe.count["pe_pv"]),)
            t = ("dve_stats", dve.count["dve_stats"])
            for j in range(TPB):
                dve.run(lambda e, j=j: e.bn_aggr(mv[:, j], st[:, j]), after=[t, last["mv"]], done="dve_aggr")
                yield
            t = ("dve_aggr", dve.count["dve_aggr"])
            last["st"] = t
            steps = [lambda e: e.tensor_tensor(rt[:, 4], mv[:, :, 0], mv[:, :, 0], ALU.mult),
                     lambda e: e.tensor_tensor(rt[:, 4], rt[:, 4], mv[:, :, 1], ALU.add)]
            steps += rsqrt_steps(rstd2, rt[:, 4], rt[:, 1], rt[:, 2], rt[:, 3])
            t = yield from slowly(steps, [t, last["rt"], ("pool_base", pool.count["pool_base"])], "dve_rsqrt")
            last["mv"] = last["rt"] = t
            yield
            for j in range(TPB):
                hr = hrow[:, (b * TPB + j) % NROW, 0:D]
                th = dve.run(lambda e, j=j, hr=hr: e.scalar_tensor_tensor(hr, hr, rstd2[:, j:j + 1], ln2_s, ALU.mult, ALU.mult), after=[t, ln2_t], done="dve_h2")
                yield from pause(2)
                i, bk, free = misc.take()

                def tr(e, bk=bk, hr=hr):
                    for k in range(KD):
                        m = e.transpose(bk[:, k * P:(k + 1) * P], hr[:, k * P:(k + 1) * P], ident)
                    return m
                tt = pe.run(tr, after=[th, *free], done="pe_h2T")
                te = act.run(lambda e, bk=bk: e.activation(h2T, bk[:, 0:KD * P].rearrange("p (k t) -> p k t", k=KD), ACT.Copy), after=[tt, last.get("h2T")], done="act_h2T")
                misc.release(i, te)
                yield from pause(2)
                i, bk, free = misc.take()

                def mm(e, bk=bk):
                    for k in range(KD):
                        m = e.matmul(bk[:, 0:NE], h2T[:, k], gate_s[:, k], start=(k == 0), stop=(k == KD - 1))
                    return m
                tt = pe.run(mm, after=[te, gate_t, *free], done="pe_gate")
                last["h2T"] = tt
                tl = dve.run(lambda e, bk=bk, j=j: e.tensor_copy(logits[:, b * TPB + j], bk[:, 0:NE]), after=[tt], done="dve_logits")
                misc.release(i, tl)
                yield
            last["logits", b] = tl
            last["h2", b] = th

        block_expert, scattered, base_landed = {}, {}, {}

        def route(gi, mem, mem_free):
            batches = GROUPS[gi]
            t0, nt, nb = batches[0] * TPB, len(batches) * TPB, n_blocks(batches)
            n8 = nt * NE
            top, idx, e1, e2, pos, tot, run_, wts, wk, small, blk = carve(mem, [8, 8, n8, n8, n8, n8, n8, 4 * nt, 2 * nt, 8 * NE, nb + 1])
            lg = logits[:, t0:t0 + nt]
            e1v, e2v, posv, totv, runv = (grid(v, nt) for v in (e1, e2, pos, tot, run_))
            wtv = wts.rearrange("p (a t) -> p a t", a=4)
            l1, l2, q1, q2 = (wtv[:, a] for a in range(4))
            n = "dve_route"
            t = dve.run(lambda e: e.memset(wk, 0.0), after=[last["logits", batches[-1]], *mem_free], done=n)
            for c in range(nt):
                t = yield from slowly([lambda e, c=c: e.max(top, lg[:, c]),
                            lambda e, c=c: e.max_index(idx.bitcast(mybir.dt.uint32), top, lg[:, c]),
                            lambda e, c=c: e.tensor_copy(wtv[:, 0:2, c], top[:, 0:2]),
                            lambda e, c=c: e.tensor_copy(wtv[:, 2:4, c], idx.bitcast(mybir.dt.uint32)[:, 0:2])], [t], n)
            iota_e = iota[:, 0:NE].unsqueeze(1).broadcast_to([P, nt, NE])
            d = wk[:, 0:nt]
            t = yield from slowly([lambda e: e.tensor_tensor(e1v, iota_e, q1.unsqueeze(2).broadcast_to([P, nt, NE]), ALU.is_equal),
                        lambda e: e.tensor_tensor(e2v, iota_e, q2.unsqueeze(2).broadcast_to([P, nt, NE]), ALU.is_equal),
                        lambda e: e.tensor_tensor(totv, e1v, e2v, ALU.add),
                        lambda e: e.tensor_copy(run_.bitcast(BF16)[:, 0:n8], tot),
                        lambda e: e.tensor_tensor(d, l2, l1, ALU.subtract)], [t, iota_t], n)
            te = act.run(lambda e: e.activation(d, d, ACT.Exp), after=[t], done="act_route")
            hot = run_.bitcast(BF16)[:, 0:n8]
            i, bk, free = misc.take()

            def mm(e, bk=bk):
                e.matmul(bk[:, 0:n8], before, hot, start=True, stop=True)
                return e.matmul(bk[:, n8:2 * n8], onesb, hot, start=True, stop=True)
            tt = pe.run(mm, after=[t, const_t, *free], done="pe_rank")
            w2c = wk[:, nt:2 * nt]
            cnt, nblk, endb, startb = (small[:, a * NE:(a + 1) * NE] for a in range(4))
            dve.run(lambda e, bk=bk: e.tensor_copy(pos, bk[:, 0:n8]), after=[tt, t], done=n)
            t = dve.run(lambda e, bk=bk: e.tensor_copy(tot, bk[:, n8:2 * n8]), after=[tt], done=n)
            misc.release(i, t)
            yield
            t = yield from slowly([lambda e: e.tensor_scalar(w2c, d, 1.0, None, ALU.add),
                        lambda e: e.reciprocal(l1, w2c),
                        lambda e: e.tensor_tensor(l2, l1, d, ALU.mult)], [te, t], n)
            ones_nt = onesf[:, 0:nt]
            t = yield from slowly([lambda e, x_=x_: e.tensor_tensor_scan(runv[:, :, x_], ones_nt, totv[:, :, x_], 0.0, ALU.mult, ALU.add) for x_ in range(NE)], [t], n)
            steps = [lambda e: e.tensor_copy(cnt, runv[:, nt - 1]),
                     lambda e: e.tensor_tensor(run_, run_, tot, ALU.subtract),
                     lambda e: e.tensor_tensor(pos, pos, run_, ALU.add)]
            per = nt
            jm = tot[:, 0:per * NE].rearrange("p (e j) -> p e j", e=NE)
            steps += [lambda e: e.tensor_tensor(jm, cnt.unsqueeze(2).broadcast_to([P, NE, per]),
                                                iota128[:, 0:per].unsqueeze(1).broadcast_to([P, NE, per]), ALU.is_gt),
                      lambda e: e.tensor_reduce(nblk, jm, AX.X, ALU.add),
                      lambda e: e.tensor_tensor_scan(endb, onesf[:, 0:NE], nblk, 0.0, ALU.mult, ALU.add),
                      lambda e: e.tensor_tensor(startb, endb, nblk, ALU.subtract),
                      lambda e: e.scalar_tensor_tensor(posv, startb.unsqueeze(1).broadcast_to([P, nt, NE]), float(P), posv, ALU.mult, ALU.add),
                      lambda e: e.tensor_tensor(e1, e1, pos, ALU.mult),
                      lambda e: e.tensor_tensor(e2, e2, pos, ALU.mult),
                      lambda e: e.tensor_reduce(q1, e1v, AX.X, ALU.add),
                      lambda e: e.tensor_reduce(q2, e2v, AX.X, ALU.add),
                      lambda e: e.tensor_copy(d.bitcast(I32), q1),
                      lambda e: e.tensor_copy(w2c.bitcast(I32), q2)]
            t = yield from slowly(steps, [t], n)
            pos_t = t
            yield
            bi = blk[0:1, 0:nb].bitcast(I32)
            acc = blk[0:1, 0:nb]
            steps = [lambda e: e.tensor_scalar(acc, iota[0:1, 0:nb], endb[0:1, 0:1], None, ALU.is_ge)]
            for x_ in range(1, NE - 1):
                steps += [lambda e, x_=x_: e.scalar_tensor_tensor(acc, iota[0:1, 0:nb], endb[0:1, x_:x_ + 1], acc, ALU.is_ge, ALU.add)]
            steps += [lambda e: e.tensor_scalar(bexp[gi], acc, float(2 * FFN), None, ALU.mult)]
            t = yield from slowly(steps, [t], n)
            block_expert[gi] = t
            got = []
            wt_t = None
            for k, (w, at) in enumerate(((l1, d), (l2, w2c))):
                if k:
                    after = [a for a in scatter.all_landed()]
                else:
                    after = []
                wt_t = dve.run(lambda e, w=w: e.tensor_copy(hrow[:, t0 % NROW:t0 % NROW + nt, D + 1], w), after=[pos_t, *after], done="dve_weight")
                for c in range(nt):
                    got.append(scatter.start(lambda e, c=c, at=at: e.indirect_dma_start(
                        rows[gi], bass.IndirectOffsetOnAxis(ap=at.bitcast(I32)[:, c:c + 1], axis=0), hrow[:, (t0 + c) % NROW, :], None),
                        after=[wt_t, *pads[gi], last["h2", batches[-1]]]))
                    yield from pause(SCATTER_PACE[gi])
            scattered[gi] = scatter.all_landed()
            last["routed", gi] = ("dve_route", dve.count["dve_route"])

        def load_w13():
            for k in range(KD):
                for e_ in range(NE):
                    last.setdefault("w13", []).append(weight_load.start(lambda e, k=k, e_=e_: e.dma_start(
                        w13_s[:, k, e_ * 2 * FFN:(e_ + 1) * 2 * FFN], w13T[k * P:(k + 1) * P, e_, :]),
                        after=projected))
                    yield

        def load_w2(experts_, after):
            for e_ in experts_:
                last.setdefault("w2", []).append(weight_load.start(lambda e, e_=e_: e.dma_start(
                    w2_mem[:, e_ * KF * D:(e_ + 1) * KF * D].rearrange("p (k n) -> p k n", k=KF), w2T[:, e_, :].rearrange("(k p) n -> p k n", p=P)), after=after))
                yield

        NBLK, NYOUT = 7, 4
        (rb, rhT, rsl, rg, rgT, ry) = carve(stack_mem, [NBLK * RW, 2 * KD * P, 2 * FFN, 2 * FFN, 2 * FFN, NYOUT * D])
        blocks = Ring([rb[:, i * RW:(i + 1) * RW] for i in range(NBLK)])
        blockT = Ring([rhT[:, i * KD * P:(i + 1) * KD * P].rearrange("p (k t) -> p k t", k=KD) for i in range(2)])
        silus = Ring([rsl[:, i * FFN:(i + 1) * FFN] for i in range(2)])
        gated = Ring([rg[:, i * FFN:(i + 1) * FFN] for i in range(2)])
        gatedT = Ring([rgT[:, i * FFN:(i + 1) * FFN] for i in range(2)])
        youts = Ring([ry[:, i * D:(i + 1) * D] for i in range(NYOUT)])
        up_banks = Ring([(bank[0], bank[1]), (bank[2], bank[3])])
        gT_banks = Ring([bank[4]])
        y_bank = Ring([bank[5]])

        def experts(work):
            first = [*last["att_done"]]
            for rg_ in (up_banks, gT_banks, y_bank, blocks, blockT, silus, gated, gatedT, youts):
                rg_.free = [tuple(first)] * len(rg_.buffers)
            n = len(work)
            got, state = {}, {}

            def fetch(w):
                gi, c = work[w]
                i, buf, free = blocks.take()
                got[w] = (i, buf, block_load.start(lambda e, gi=gi, c=c, buf=buf: e.dma_start(buf, rows[gi][c * P:(c + 1) * P, :]),
                                                  after=[*free, *scattered[gi]]))

            def turn(w):
                i, buf, ready = got[w]
                im, bk, free = misc.take()

                def tr(e):
                    for k in range(KD):
                        m = e.transpose(bk[:, k * P:(k + 1) * P], buf[:, k * P:(k + 1) * P], ident)
                    return m
                tt = pe.run(tr, after=[ready, *free], done="pe_blockT")
                ib, bT, bfree = blockT.take()
                te = dve.run(lambda e: e.tensor_copy(bT, bk[:, 0:KD * P].rearrange("p (k t) -> p k t", k=KD)), after=[tt, *bfree], done="dve_blockT")
                misc.release(im, te)
                turned[w] = (ib, bT, te)

            def up(w, half):
                gi, c = work[w]
                if half == 0:
                    iu, banks, free = up_banks.take()
                    ups[w] = (iu, banks)
                iu, banks = ups[w]
                ib, bT, te = turned[w]

                def mm(e):
                    if half == 0:
                        offs[w] = e.value_load(bexp[gi][0:1, c:c + 1], min_val=0, max_val=(NE - 1) * 2 * FFN)
                    for k in range(KD):
                        m = e.matmul(banks[half], bT[:, k], w13_s[:, k, bass.ds(offs[w] + half * FFN, FFN)], start=(k == 0), stop=(k == KD - 1))
                    return m
                tt = pe.run(mm, after=[te, block_expert[gi], *last["w13"], *(free if half == 0 else ())], done="pe_up")
                if half == 0:
                    isl, sl, sfree = silus.take()
                    ts = act.run(lambda e: e.activation(sl, banks[0], ACT.Silu), after=[tt, *sfree], done="act_silu")
                    state[w] = (isl, sl, ts)
                else:
                    isl, sl, ts = state[w]
                    blockT.release(ib, tt)
                    ig, g_, gfree = gated.take()
                    tg = dve.run(lambda e: e.tensor_tensor(g_, banks[1], sl, ALU.mult), after=[ts, tt, *gfree], done="dve_gated")
                    silus.release(isl, tg)
                    up_banks.release(iu, ts, tg)
                    state[w] = (ig, g_, tg)

            def turn_gated(w):
                ig, g_, tg = state[w]
                i, bk, free = gT_banks.take()

                def tr(e):
                    for k in range(KF):
                        m = e.transpose(bk[:, k * P:(k + 1) * P], g_[:, k * P:(k + 1) * P], ident)
                    return m
                tt = pe.run(tr, after=[tg, *free], done="pe_gatedT")
                gated.release(ig, tt)
                it, gT, tfree = gatedT.take()
                te = act.run(lambda e: e.activation(gT, bk, ACT.Copy), after=[tt, *tfree], done="act_gatedT")
                gT_banks.release(i, te)
                state[w] = (it, gT, te)

            def down(w):
                gi, c = work[w]
                it, gT, te = state[w]
                ib, buf, _ = got[w]
                i, bk, free = y_bank.take()

                def mm(e):
                    v = offs[w]
                    for k in range(KF):
                        m = e.matmul(bk[:, 0:D], gT[:, k * P:(k + 1) * P], w2_mem[:, bass.ds(v + k * D, D)], start=(k == 0), stop=(k == KF - 1))
                    return m
                tt = pe.run(mm, after=[te, *last["w2"], *free], done="pe_down")
                gatedT.release(it, tt)
                iy, y, yfree = youts.take()
                ty = dve.run(lambda e: e.tensor_scalar(y, bk[:, 0:D], buf[:, D + 1:D + 2], None, ALU.mult), after=[tt, *yfree], done="dve_y")
                y_bank.release(i, ty)
                ta = add_out.start(lambda e: e.indirect_dma_start(
                    out_rows, bass.IndirectOffsetOnAxis(ap=buf.bitcast(I32)[:, D:D + 1], axis=0), y, None,
                    bounds_check=NBATCH * SEQ - 1, oob_is_err=False, compute_op=ALU.add), after=[ty, *base_landed[GROUPS[gi][-1]]])
                youts.release(iy, ta)
                blocks.release(ib, ta, ty)
            offs, ups, turned = {}, {}, {}
            for w in range(4):
                fetch(w)
            turn(0)
            for w in range(n + 1):
                if w < n:
                    up(w, 0)
                    yield w
                if w >= 1:
                    turn_gated(w - 1)
                if w + 1 < n:
                    turn(w + 1)
                if w < n:
                    yield w
                    up(w, 1)
                    yield w
                if w >= 1:
                    down(w - 1)
                if w + 4 < n:
                    fetch(w + 4)
                yield w

        bexp = [sb(f"bexp{i}", [1, n_blocks(g)], I32) for i, g in enumerate(GROUPS)]

        def drain(g):
            for _ in g:
                pass

        def chain(*gs):
            for g in gs:
                yield from g

        EARLY = sum(f.shape[1] for f in (wgT_f, pair_f, wqkv_f, x_even, v_even, rot3, rot4)) // (KF * D)

        def weights():
            yield from load_w13()
            while NBATCH - 2 not in base_landed:
                yield
            yield from load_w2(range(EARLY), [*x1_free[0], *v1_free[0], *projected])

        def closing(b):
            while len(pack_ready[b]) < NKV * QR:
                yield
            yield from pause(PACK_PACE)
            yield from close(b)

        def advance_norms():
            for q in list(norms):
                if next(q, 0) == 0:
                    norms.remove(q)

        def rest_of(g):
            for _ in g:
                pass
            return
            yield

        def sides(b):
            if b:
                yield from closing(b - 1)
            if b + 1 < NBATCH:
                yield from project(b + 1)
            else:
                yield from route(0, route_a, pads[0] + pads[1])
                yield from load_w2(range(EARLY, NE), [last["routed", 0], *scattered[0], *projected])

        groups = [(b, g) for b in range(NBATCH) for g in range(NKV)]
        for at in project(0):
            if at == "xn":
                const_t, wq_ready = dve_prepare()
            if isinstance(at, tuple):
                load_first_stack(at[1])
        load_stack(0, 1)
        filling = fill_rows()
        drain(max_pass(0, 0, 0))
        late = max_pass(0, 0, 1)
        for _ in range(LATE_STEPS):
            next(late)
        for n, (b, g) in enumerate(groups):
            if (b, g) == (NBATCH - 1, 0):
                projected = [(name, pe.count[name]) for name in ("pe_square", "pe_v", "pe_qk")] + \
                            [("pool_split", pool.count["pool_split"]), ("dve_rope", dve.count["dve_rope"]), *split_store.all_landed()]
                background = weights()
            if g == 0:
                side, side_rate = sides(b), SIDE.get(b, SIDE_ELSE)
            assert b + 1 < NBATCH or sum(map(len, pads)) == -(-n_blocks(GROUPS[0]) // PAD_BLOCKS) - (-n_blocks(GROUPS[1]) // PAD_BLOCKS), "padding not complete"
            work = chain(*(attend(b, g, r) for r in range(QR))) if n else chain(attend(b, g, 0), rest_of(late), attend(b, g, 1))
            ahead = chain(*(max_pass(*groups[n + 1], r) for r in range(QR))) if n + 1 < len(groups) else iter(())
            ahead_due = side_due = 0.0
            for k, _ in enumerate(work):
                if n == 0 and next(late, 0) is None and next(late, 0) is None:
                    continue
                if b == NBATCH - 1 and k % WEIGHT_PACE == 0:
                    next(background, None)
                if k % PAD_PACE == 0:
                    next(filling, None)
                ahead_due += AHEAD
                side_due += side_rate
                while ahead_due >= 1:
                    next(ahead, None)
                    ahead_due -= 1
                while side_due >= 1:
                    next(side, None)
                    side_due -= 1
                advance_norms()
                if k == STACK_STEP and n + 2 < len(groups):
                    if groups[n + 2][0] > b and b + 1 < NBATCH:
                        drain(side)
                    load_stack(*groups[n + 2])
            drain(ahead)
        while held:
            held.pop(0)()
        drain(side)
        drain(background)
        last["att_done"] = [(k, pe.count[k]) for k in ("pe_pv", "pe_scores", "pe_max")] + \
                           [(k, act.count[k]) for k in ("act_pv", "act_exp")] + [("dve_max", dve.count["dve_max"])]
        last["att_done"] += [t for ticks in misc.free for t in ticks]
        misc = Ring([bank[6], bank[7]])
        misc.free = [tuple(last["att_done"])] * 2
        side = chain(closing(NBATCH - 1), route(1, probs_mem, last["att_done"]))
        n_first, side_due = n_blocks(GROUPS[0]), 0.0
        every = [(0, c) for c in range(n_first)] + [(1, c) for c in range(n_blocks(GROUPS[1]))]
        for w in experts(every):
            advance_norms()
            side_due += SIDE_EXPERTS
            while side_due >= 1 and w < n_first - SPARE_BLOCKS:
                next(side, None)
                side_due -= 1
            if w >= n_first - SPARE_BLOCKS:
                assert next(side, 0) == 0, "the second group's rows come too late"
        pool.wait(*add_out.all_landed())
        sp.wait(*add_out.all_landed(), *base_store.all_landed())

        block = ctx.enter_context(nc.Block())

        @block.sync
        def _(e):
            sp.play(e)

        @block.gpsimd
        def _(e):
            pool.play(e)

        @block.scalar
        def _(e):
            act.play(e)

        @block.vector
        def _(e):
            dve.play(e)

        @block.tensor
        def _(e):
            pe.play(e)


def rope_tables():
    inv_freq = (np.float32(1.0) / np.power(np.float32(THETA), np.arange(0, HD, 2, dtype=np.float32) / np.float32(HD))).astype(np.float32)
    freqs = (np.arange(SEQ, dtype=np.float32)[:, None] * inv_freq[None, :]).T
    cos, sin = np.cos(freqs), np.sin(freqs)
    q = np.stack([np.repeat(a, NH, axis=0) for a in (cos, sin)])
    k = np.stack([np.repeat(np.concatenate(a), NKV, axis=0) for a in ((cos, cos), (-sin, sin))])
    return np.ascontiguousarray(q), np.ascontiguousarray(k)


def kernel(L0_attn_x, L0_attn_W_theta, L0_attn_W_phi, L0_attn_W_g, L0_ffn_ln1_w, L0_ffn_ln2_w,
           L0_ffn_wqkv, L0_ffn_wo, L0_ffn_gate_w, L0_ffn_w13, L0_ffn_w2):
    import concourse.bacc as bacc
    from concourse.bass_utils import run_bass_kernel_spmd

    def lay(a):
        return np.ascontiguousarray(np.asarray(a))

    wqkv = np.asarray(L0_ffn_wqkv)
    heads = np.arange(QK).reshape(-1, HD)
    order = np.concatenate([heads[:NH].T.reshape(-1), heads[NH:].T.reshape(-1), np.arange(QK, QKV)])
    rope_q, rope_k = rope_tables()
    tri = np.stack([np.triu(np.ones((P, P), np.float32), 1)] * 2, axis=1)
    ids = np.arange(NTILE * P, dtype=np.int32).reshape(NTILE, P).T
    arrays = {
        "x": lay(L0_attn_x), "wtheta": lay(L0_attn_W_theta), "wphi": lay(L0_attn_W_phi), "wgT": lay(np.asarray(L0_attn_W_g).T),
        "ln1": lay(L0_ffn_ln1_w), "ln2": lay(L0_ffn_ln2_w), "wqkvT": lay(wqkv[order].T),
        "woT": lay(np.asarray(L0_ffn_wo).T), "gateT": lay(np.asarray(L0_ffn_gate_w).T),
        "w13T": lay(np.asarray(L0_ffn_w13).transpose(2, 0, 1)), "w2T": lay(np.asarray(L0_ffn_w2).transpose(2, 0, 1)),
        "rope_q": rope_q, "rope_k": rope_k, "eye": np.eye(P, dtype=np.float32), "tri": lay(tri), "ids": lay(ids),
    }
    nc = bacc.Bacc("TRN2", target_bir_lowering=False, num_devices=1)
    ins = {f"in_{k}": v for k, v in arrays.items()}
    args = [nc.dram_tensor(k, v.shape, mybir.dt.from_np(v.dtype), kind="ExternalInput").ap() for k, v in ins.items()]
    out = nc.dram_tensor("out_0", [NBATCH, SEQ, D], F32, kind="ExternalOutput").ap()
    mega_kernel(nc, *args, out)
    r = run_bass_kernel_spmd(nc, [ins], core_ids=[0])
    return r.results[0]["out_0"]
```
